# Optimizing a Trainium2 kernel written in Bass

```python
import numpy as np
import jax
import jax.numpy as jnp

def _softmax(x, axis=-1):
    return jax.nn.softmax(x, axis=axis)

def _gelu(x):
    return jax.nn.gelu(x, approximate=True)

def _silu(x):
    return jax.nn.silu(x)

def _sigmoid(x):
    return jax.nn.sigmoid(x)

def _layernorm(x, axis=-1, eps=1e-05):
    m = jnp.mean(x, axis=axis, keepdims=True)
    v = jnp.var(x, axis=axis, keepdims=True)
    return (x - m) / jnp.sqrt(v + eps)

def _scatter_add(tgt, idx, src, axis=0):
    return tgt.at[idx].add(src)

def _segment_sum(src, seg, n):
    return jax.ops.segment_sum(src, seg, n)
kernel_name = 'mk_hybrid_d1_jaxref_r4_7e269e'

def setup_inputs(seed: int=0):
    np.random.seed(seed)
    _w = jnp.asarray

    def _L0_attn_a_setup():
        import jax, jax.numpy as jnp
        import numpy as np
        import math
        N_HEAD = 16
        HEAD_QKV = 256
        WM_DECAY_LENGTH = 512
        WM_DECAY_RATE = 1.0
        WM_ECHOIC = 16

        def decay_weight_matrix(n):
            dl = WM_DECAY_LENGTH - WM_ECHOIC + 1
            nums = jnp.linspace(0.0, 1.0, dl)
            decay_values = 1.0 - jnp.power(nums, 1.0 / (np.e * WM_DECAY_RATE))
            decay_values = jnp.concatenate([jnp.ones(WM_ECHOIC - 1), decay_values])
            decay_values = decay_values[:n]
            idx = jnp.arange(n)[:, None] - jnp.arange(n)[None, :]
            mat = decay_values[jnp.clip(idx, 0, n - 1)]
            return jnp.tril(mat).astype(jnp.float32)
        key = jax.random.key(seed)
        k1, k2, k3 = jax.random.split(key, 3)
        B, T, C = (2, 512, 256)
        x = jax.random.normal(k1, (B, T, C), dtype=jnp.float32)
        W_attn = jax.random.normal(k2, (C, 3 * HEAD_QKV), dtype=jnp.float32) * (1.0 / math.sqrt(C))
        W_proj = jax.random.normal(k3, (HEAD_QKV, C), dtype=jnp.float32) * (1.0 / math.sqrt(HEAD_QKV))
        return {'x': x, 'W_attn': W_attn, 'W_proj': W_proj}
    _L0_attn_a_in = _L0_attn_a_setup()

    def _L0_attn_b_setup():
        import jax, jax.numpy as jnp
        import numpy as np
        import math
        H = 16
        N_EMBD = 256
        EPS = 1e-05
        key = jax.random.key(seed)
        ks = jax.random.split(key, 6)
        B, T, C = (2, 512, 256)
        x = jax.random.normal(ks[0], (B, T, C), dtype=jnp.float32)
        s = 0.02
        Wq = jax.random.normal(ks[1], (C, N_EMBD), dtype=jnp.float32) * s
        Wk = jax.random.normal(ks[2], (C, N_EMBD), dtype=jnp.float32) * s
        Wv = jax.random.normal(ks[3], (C, N_EMBD), dtype=jnp.float32) * s
        Wo = jax.random.normal(ks[4], (N_EMBD, C), dtype=jnp.float32) * s
        return {'x': x, 'Wq': Wq, 'bq': jnp.zeros((N_EMBD,), jnp.float32), 'Wk': Wk, 'bk': jnp.zeros((N_EMBD,), jnp.float32), 'Wv': Wv, 'bv': jnp.zeros((N_EMBD,), jnp.float32), 'Wo': Wo, 'bo': jnp.zeros((C,), jnp.float32), 'gamma': jnp.ones((C,), jnp.float32), 'beta': jnp.zeros((C,), jnp.float32)}
    _L0_attn_b_in = _L0_attn_b_setup()

    def _L0_ffn_setup():
        import jax, jax.numpy as jnp
        import numpy as np

        def _binarize(w):
            alpha = jax.lax.stop_gradient(jnp.mean(jnp.abs(w), axis=1, keepdims=True))
            bw = alpha * jnp.sign(w)
            return w + jax.lax.stop_gradient(bw - w)
        key = jax.random.key(seed)
        k1, k2, k3, k4, k5 = jax.random.split(key, 5)
        D, H = (256, 1024)
        x = jax.random.normal(k1, (64, 196, D), dtype=jnp.float32)
        w1 = jax.random.normal(k2, (H, D), dtype=jnp.float32) * 0.02
        b1 = jax.random.normal(k3, (H,), dtype=jnp.float32) * 0.02
        w2 = jax.random.normal(k4, (D, H), dtype=jnp.float32) * 0.02
        b2 = jax.random.normal(k5, (D,), dtype=jnp.float32) * 0.02
        return {'x': x, 'w1': w1, 'b1': b1, 'w2': w2, 'b2': b2}
    _L0_ffn_in = _L0_ffn_setup()
    _d = {'L0_attn_a_x': _L0_attn_a_in['x'], 'L0_attn_a_W_attn': _L0_attn_a_in['W_attn'], 'L0_attn_a_W_proj': _L0_attn_a_in['W_proj'], 'L0_attn_b_Wq': _L0_attn_b_in['Wq'], 'L0_attn_b_bq': _L0_attn_b_in['bq'], 'L0_attn_b_Wk': _L0_attn_b_in['Wk'], 'L0_attn_b_bk': _L0_attn_b_in['bk'], 'L0_attn_b_Wv': _L0_attn_b_in['Wv'], 'L0_attn_b_bv': _L0_attn_b_in['bv'], 'L0_attn_b_Wo': _L0_attn_b_in['Wo'], 'L0_attn_b_bo': _L0_attn_b_in['bo'], 'L0_attn_b_gamma': _L0_attn_b_in['gamma'], 'L0_attn_b_beta': _L0_attn_b_in['beta'], 'L0_ffn_w1': _L0_ffn_in['w1'], 'L0_ffn_b1': _L0_ffn_in['b1'], 'L0_ffn_w2': _L0_ffn_in['w2'], 'L0_ffn_b2': _L0_ffn_in['b2']}
    _x0 = _d['L0_attn_a_x']
    _d['L0_attn_a_x'] = jax.random.normal(jax.random.fold_in(jax.random.key(seed), 1), (2, 2048, 256), dtype=_x0.dtype)
    del _x0
    return _d

def reference(L0_attn_a_x, L0_attn_a_W_attn, L0_attn_a_W_proj, L0_attn_b_Wq, L0_attn_b_bq, L0_attn_b_Wk, L0_attn_b_bk, L0_attn_b_Wv, L0_attn_b_bv, L0_attn_b_Wo, L0_attn_b_bo, L0_attn_b_gamma, L0_attn_b_beta, L0_ffn_w1, L0_ffn_b1, L0_ffn_w2, L0_ffn_b2):

    def _L0_attn_a_ref(x, W_attn, W_proj):
        import jax, jax.numpy as jnp
        import numpy as np
        import math
        N_HEAD = 16
        HEAD_QKV = 256
        WM_DECAY_LENGTH = 512
        WM_DECAY_RATE = 1.0
        WM_ECHOIC = 16

        def decay_weight_matrix(n):
            dl = WM_DECAY_LENGTH - WM_ECHOIC + 1
            nums = jnp.linspace(0.0, 1.0, dl)
            decay_values = 1.0 - jnp.power(nums, 1.0 / (np.e * WM_DECAY_RATE))
            decay_values = jnp.concatenate([jnp.ones(WM_ECHOIC - 1), decay_values])
            decay_values = decay_values[:n]
            idx = jnp.arange(n)[:, None] - jnp.arange(n)[None, :]
            mat = decay_values[jnp.clip(idx, 0, n - 1)]
            return jnp.tril(mat).astype(jnp.float32)
        B, T, C = x.shape
        hd = HEAD_QKV // N_HEAD
        qkv = x @ W_attn
        q, k, v = jnp.split(qkv, 3, axis=-1)
        q = q.reshape(B, T, N_HEAD, hd).transpose(0, 2, 1, 3)
        k = k.reshape(B, T, N_HEAD, hd).transpose(0, 2, 1, 3)
        v = v.reshape(B, T, N_HEAD, hd).transpose(0, 2, 1, 3)
        att = jnp.einsum('bhqd,bhkd->bhqk', q, k) * (1.0 / math.sqrt(hd))
        causal = jnp.tril(jnp.ones((T, T), dtype=bool))
        att = jnp.where(causal, att, -jnp.inf)
        att = jax.nn.softmax(att, axis=-1)
        att = att * decay_weight_matrix(T)
        y = jnp.einsum('bhqk,bhkd->bhqd', att, v)
        y = y.transpose(0, 2, 1, 3).reshape(B, T, HEAD_QKV)
        return y @ W_proj

    def _L0_attn_b_ref(x, Wq, bq, Wk, bk, Wv, bv, Wo, bo, gamma, beta):
        import jax, jax.numpy as jnp
        import numpy as np
        import math
        H = 16
        N_EMBD = 256
        EPS = 1e-05
        B, T, _ = x.shape
        Dh = N_EMBD // H

        def split_heads(y):
            return y.reshape(B, T, H, Dh).transpose(0, 2, 1, 3)
        q = split_heads(x @ Wq + bq)
        k = split_heads(x @ Wk + bk)
        v = split_heads(x @ Wv + bv)
        att = jnp.einsum('bhtd,bhsd->bhts', q, k) * (1.0 / math.sqrt(Dh))
        causal = jnp.tril(jnp.ones((T, T), dtype=bool))
        att = jnp.where(causal[None, None], att, -jnp.inf)
        att = jax.nn.softmax(att, axis=-1)
        o = jnp.einsum('bhts,bhsd->bhtd', att, v)
        o = o.transpose(0, 2, 1, 3).reshape(B, T, N_EMBD)
        y = o @ Wo + bo
        mu = jnp.mean(y, axis=-1, keepdims=True)
        var = jnp.var(y, axis=-1, keepdims=True)
        return (y - mu) * jax.lax.rsqrt(var + EPS) * gamma + beta

    def _L0_ffn_ref(x, w1, b1, w2, b2):
        import jax, jax.numpy as jnp
        import numpy as np

        def _binarize(w):
            alpha = jax.lax.stop_gradient(jnp.mean(jnp.abs(w), axis=1, keepdims=True))
            bw = alpha * jnp.sign(w)
            return w + jax.lax.stop_gradient(bw - w)
        bw1 = _binarize(w1)
        h = jnp.einsum('bsd,hd->bsh', x, bw1) + b1
        h = jax.nn.gelu(h, approximate=False)
        bw2 = _binarize(w2)
        out = jnp.einsum('bsh,dh->bsd', h, bw2) + b2
        return out
    x = L0_attn_a_x
    x = x + _L0_attn_a_ref(_layernorm(x, axis=-1), L0_attn_a_W_attn, L0_attn_a_W_proj)
    x = x + _L0_ffn_ref(_layernorm(x, axis=-1), L0_ffn_w1, L0_ffn_b1, L0_ffn_w2, L0_ffn_b2)
    x = x + _L0_attn_b_ref(_layernorm(x, axis=-1), L0_attn_b_Wq, L0_attn_b_bq, L0_attn_b_Wk, L0_attn_b_bk, L0_attn_b_Wv, L0_attn_b_bv, L0_attn_b_Wo, L0_attn_b_bo, L0_attn_b_gamma, L0_attn_b_beta)
    x = x + _L0_ffn_ref(_layernorm(x, axis=-1), L0_ffn_w1, L0_ffn_b1, L0_ffn_w2, L0_ffn_b2)
    return x

_drawn_inputs = setup_inputs


def setup_inputs(seed=0):
    import zlib

    import numpy as np

    out = dict(_drawn_inputs(seed))
    spreads = {'L0_attn_b_bq': (0.0, 0.8),
     'L0_attn_b_bk': (0.0, 0.8),
     'L0_attn_b_bv': (0.0, 0.1),
     'L0_attn_b_bo': (0.0, 0.1),
     'L0_attn_b_gamma': (1.0, 0.2),
     'L0_attn_b_beta': (0.0, 0.1)}
    factors = {'L0_attn_b_Wq': 8.0, 'L0_attn_b_Wk': 8.0, 'L0_ffn_b1': 7.072}
    for name, (base, spread) in spreads.items():
        noise = np.random.default_rng([zlib.crc32(name.encode()), seed]).standard_normal(out[name].shape)
        drawn = base * np.exp(spread * noise) if base else spread * noise
        out[name] = jnp.asarray(drawn.astype(out[name].dtype))
    for name, factor in factors.items():
        out[name] = (out[name] * factor).astype(out[name].dtype)
    return out
```

```python
from contextlib import ExitStack

import numpy as np
import concourse.bass as bass
from concourse import mybir

ALU = mybir.AluOpType
ACT = mybir.ActivationFunctionType
AX = mybir.AxisListType
F32 = mybir.dt.float32
F32R = mybir.dt.float32r
BF16 = mybir.dt.bfloat16

P = 128
B, T, D = 2, 2048, 256
H, HD = 16, 16
FF = 1024
KT = D // P
HT = FF // P
CH = 512
NC = T // CH
TB = CH // P
GH = 4
NG = H // GH
GROUPS = B * NG
STRIP = P // GH
BLOCKS = T // P
SCALE = HD ** -0.5
EPS = 1e-5
MASK = -1e37
PAIRS = 4
MROW = PAIRS * HD
ECHOIC, DECAY_LENGTH = 16, 512
SPAN = DECAY_LENGTH - 1
BAND = SPAN // P + 1
DECAY_COLS = (BAND + 1) * P
MBANKS, EBANKS = 3, 3


def decay_table():
    dl = DECAY_LENGTH - ECHOIC + 1
    nums = np.linspace(0.0, 1.0, dl, dtype=np.float32)
    values = (1.0 - np.power(nums, np.float32(1.0 / np.e))).astype(np.float32)
    values = np.concatenate([np.ones(ECHOIC - 1, np.float32), values])
    lag = np.arange(DECAY_COLS)[None, :] - np.arange(P)[:, None]
    return np.where(lag < 0, 0, values[np.clip(lag, 0, DECAY_LENGTH - 1)]).astype(np.float32)


def row_of(vector):
    return vector.rearrange("(a n) -> a n", a=1)


def columns_of(vector):
    return vector.rearrange("(t p) -> p t", p=P)


def phase_semaphores(nc, ctx, name):
    taken = []

    def give_back():
        nc.clear_and_free_semaphores(taken)
        nc.all_engine_barrier()

    def take(n):
        taken.append(nc.alloc_semaphore(name=f"{name}_{n}"))
        return taken[-1]

    ctx.callback(give_back)
    return take


def setup(nc, io, keep):
    with ExitStack() as ctx:
        sb = lambda n, s, d: ctx.enter_context(nc.sbuf_tensor(n, s, d))
        w1 = sb("w1_rows", [P, HT, D], F32)
        w2 = sb("w2_rows", [P, KT, FF], F32)
        neg = sb("w_negative", [P, HT, D], F32)
        sign1 = sb("w1_sign", [P, HT, D], F32)
        sign2 = sb("w2_sign", [P, KT, FF], F32)
        turned = ctx.enter_context(nc.psum_tensor("w_turned", [P, 4, CH], F32))
        sem = phase_semaphores(nc, ctx, "setup")
        w_loaded, ident_ready, zeroed = sem("w_loaded"), sem("ident_ready"), sem("zeroed")
        sign_step, signs_ready = sem("sign_step"), sem("signs_ready")
        w_turned, w_kept = sem("w_turned_sem"), sem("w_kept")
        const_loaded = sem("const_loaded")
        ident, identb = keep["ident"], keep["identb"]
        block = ctx.enter_context(nc.Block())

        @block.sync
        def _(sp):
            sp.dma_start(w1[:, :, :], io["w1"].rearrange("(t p) d -> p t d", p=P)).then_inc(w_loaded, 16)
            sp.dma_start(w2[:, :, :], io["w2"].rearrange("(t p) d -> p t d", p=P)).then_inc(w_loaded, 16)
            with nc.allow_non_contiguous_dma(reason="biases as columns, once"):
                sp.dma_start(keep["b1"][:, :], columns_of(io["b1"])).then_inc(const_loaded, 16)
                sp.dma_start(keep["b2"][:, :], columns_of(io["b2"])).then_inc(const_loaded, 16)
            sp.dma_start(keep["decay"][:, :], io["decay"]).then_inc(const_loaded, 16)
            sp.wait_ge(const_loaded, 48)

        @block.gpsimd
        def _(pool):
            pool.memset(ident[:, :], 0.0).then_inc(zeroed, 1)
            pool.memset(identb[:, :], 0.0).then_inc(zeroed, 1)
            pool.memset(keep["mask_q"][:, :], 0.0).then_inc(zeroed, 1)
            pool.memset(keep["mask_k"][:, :], 0.0).then_inc(zeroed, 1)
            pool.memset(keep["spread"][:, :], 0.0).then_inc(zeroed, 1)
            pool.memset(keep["ones_strip"][:, 0:HD], 0.0).then_inc(zeroed, 1)
            pool.memset(keep["ones_strip"][:, HD:STRIP], 1.0).then_inc(zeroed, 1)
            pool.wait_ge(zeroed, 7)
            for m in (ident, identb):
                pool.affine_select(out=m[:, :], in_=m[:, :], compare_op=ALU.not_equal, fill=1.0, base=0,
                                   pattern=[[-1, P]], channel_multiplier=1).then_inc(ident_ready, 1)
            pool.affine_select(out=keep["mask_q"][:, :], in_=keep["mask_q"][:, :], compare_op=ALU.is_ge,
                               fill=MASK, base=0, pattern=[[-1, P]], channel_multiplier=1).then_inc(ident_ready, 1)
            pool.affine_select(out=keep["mask_k"][:, :], in_=keep["mask_k"][:, :], compare_op=ALU.is_ge,
                               fill=MASK, base=0, pattern=[[1, P]], channel_multiplier=-1).then_inc(ident_ready, 1)
            for j in range(GH):
                s = keep["spread"][:, j * STRIP:(j + 1) * STRIP]
                pool.affine_select(out=s, in_=s, compare_op=ALU.not_equal, fill=1.0, base=-(j * STRIP + HD),
                                   pattern=[[0, STRIP]], channel_multiplier=1).then_inc(ident_ready, 1)

        @block.vector
        def _(dve):
            dve.wait_ge(w_loaded, 32)
            for w, s, n, tiles, alpha in ((w1, sign1, D, HT, keep["alpha1"]), (w2, sign2, FF, KT, keep["alpha2"])):
                step = 4 * (w is w2)
                below = neg[:, :, :].rearrange("p a b -> p (a b)").rearrange("p (t d) -> p t d", t=tiles)
                dve.tensor_reduce(alpha[:, :], w[:, :, :], AX.X, ALU.add,
                                  apply_absolute_value=True).then_inc(sign_step, 1)
                dve.wait_ge(sign_step, step + 1)
                dve.tensor_scalar(alpha[:, :], alpha[:, :], 1.0 / n, None, ALU.mult).then_inc(sign_step, 1)
                dve.wait_ge(sign_step, step + 2)
                dve.tensor_scalar(below, w[:, :, :], 0.0, None, ALU.is_lt).then_inc(sign_step, 1)
                dve.wait_ge(sign_step, step + 3)
                dve.scalar_tensor_tensor(out=s[:, :, :], in0=w[:, :, :], scalar=0.0, in1=below,
                                         op0=ALU.is_gt, op1=ALU.subtract).then_inc(sign_step, 1)
                dve.wait_ge(sign_step, step + 4)
            dve.sem_inc(signs_ready, 1)
            for n in range(8):
                dve.wait_ge(w_turned, n + 1)
                if n < 4:
                    kt, half = n // 2, n % 2
                    dst = keep["w1s"][:, kt, half * CH:(half + 1) * CH]
                    dve.tensor_copy(dst, turned[:, n % 4, :]).then_inc(w_kept, 1)
                else:
                    ht = 2 * (n - 4)
                    dst = keep["w2s"][:, ht:ht + 2, :]
                    dve.tensor_copy(dst, turned[:, n % 4, :].rearrange("p (a d) -> p a d", a=2)).then_inc(w_kept, 1)

        @block.tensor
        def _(pe):
            pe.wait_ge(ident_ready, 1)
            pe.wait_ge(signs_ready, 1)
            for n in range(8):
                if n >= 4:
                    pe.wait_ge(w_kept, n - 3)
                for q in range(4):
                    if n < 4:
                        kt, half = n // 2, n % 2
                        src = sign1[:, 4 * half + q, kt * P:(kt + 1) * P]
                    else:
                        ht = 2 * (n - 4) + q // 2
                        src = sign2[:, q % 2, ht * P:(ht + 1) * P]
                    mm = pe.transpose(turned[:, n % 4, q * P:(q + 1) * P], src, ident[:, :])
                mm.then_inc(w_turned, 1)


def halves_sums(dve, stats, mean, half):
    dve.tensor_tensor(mean, stats[:, :, 1], stats[:, :, 4], ALU.add)
    dve.tensor_tensor(half[:, 0, :], stats[:, :, 1], stats[:, :, 4], ALU.subtract)
    return dve.tensor_tensor(half[:, 1, :], stats[:, :, 2], stats[:, :, 5], ALU.add)


def halves_terms(dve, mean, half):
    dve.tensor_scalar(mean, mean, 0.5, None, ALU.mult)
    dve.tensor_tensor(half[:, 0, :], half[:, 0, :], half[:, 0, :], ALU.mult)
    return dve.tensor_scalar(half[:, 1, :], half[:, 1, :], 1.0 / D, EPS, ALU.mult, ALU.add)


def halves_variance(dve, var, half):
    return dve.scalar_tensor_tensor(out=var, in0=half[:, 0, :], scalar=0.25, in1=half[:, 1, :],
                                    op0=ALU.mult, op1=ALU.add)


def projections(nc, name, x_dram, weights, biases, v_ones, keep, dram):
    with ExitStack() as ctx:
        sb = lambda n, s, d: ctx.enter_context(nc.sbuf_tensor(f"{name}_{n}", s, d))
        ps = lambda n, s: ctx.enter_context(nc.psum_tensor(f"{name}_{n}", s, F32))
        sm = phase_semaphores(nc, ctx, name)
        wqkv = sb("wqkv", [P, KT, 3 * D], F32)
        bqk = sb("bqk", [P, 2 * KT], F32)
        bv = sb("bv", [P, D], F32)
        x = sb("x", [P, 2, TB, D], F32)
        xn = sb("xn", [P, 2, TB, D], F32)
        xt = sb("xt", [P, 2, KT, CH], F32)
        stats = sb("stats", [P, 2, TB, 6], F32)
        mean, half = sb("mean", [P, 2, TB], F32), sb("half", [P, 2, TB], F32)
        var = sb("var", [P, 2, TB], F32)
        sd = sb("sd", [P, 2, TB], F32)
        rs = sb("rs", [P, 2, TB], F32)
        qk_hi = sb("qk_hi", [P, 2, 2 * KT, CH], F32R)
        qk_lo = sb("qk_lo", [P, 2, 2 * KT, CH], F32R)
        vt = sb("vt", [P, 2, TB, H, STRIP], F32)
        pt = ps("pt", [P, KT, CH])
        pqk = ps("pqk", [P, 2 * KT, CH])
        pv = ps("pv", [P, TB, D])
        w_in, x_in, chain = sm("w_in"), [sm("x_in0"), sm("x_in1")], sm("chain")
        var_ready, sd_ready, xn_ready = sm("var_ready"), sm("sd_ready"), sm("xn_ready")
        turned, xt_ready, qk_done, v_done = sm("turned"), sm("xt_ready"), sm("qk_done"), sm("v_done")
        hi_ready, lo_ready, v_kept, vt_filled = sm("hi_ready"), sm("lo_ready"), sm("v_kept"), sm("vt_filled")
        stored = [sm(f"stored{i}") for i in range(2)]
        block = ctx.enter_context(nc.Block())
        M = 2 * KT
        STORE = 16 * (8 + NG)
        N_W = 16 * (len(weights) + 3 * bool(biases))

        @block.sync
        def _(sp):
            for src, (a, z) in weights:
                sp.dma_start(wqkv[:, :, a:z], src.rearrange("(t p) n -> p t n", p=P)).then_inc(w_in, 16)
            if biases:
                with nc.allow_non_contiguous_dma(reason="biases as columns, once"):
                    sp.dma_start(bqk[:, 0:KT], columns_of(biases[0])).then_inc(w_in, 16)
                    sp.dma_start(bqk[:, KT:M], columns_of(biases[1])).then_inc(w_in, 16)
                sp.dma_start(bv[:, :], row_of(biases[2]).to_broadcast([P, D])).then_inc(w_in, 16)
            for par in range(2):
                sp.sem_inc(stored[par], STORE)

            def store(b, c):
                G, par = NC * b + c, c % 2
                sp.wait_ge(hi_ready, M * G + M)
                sp.wait_ge(lo_ready, M * G + 2 * M)
                for hl, t in ((0, qk_hi), (1, qk_lo)):
                    for a in range(2):
                        for qk in range(2):
                            dst = dram["qk"][b, :, hl, qk, :, c * CH:(c + 1) * CH]
                            dst = dst.rearrange("(m a) p t -> a p m t", a=2)[a]
                            sp.dma_start(dst, t[64 * a:64 * a + 64, par, KT * qk:KT * qk + KT, :].bitcast(F32))\
                              .then_inc(stored[par], 16)
                sp.wait_ge(v_kept, G + 2)
                for gh in range(NG):
                    sp.dma_start(dram["v"][b, gh, c].rearrange("p (t j e) -> p t j e", t=TB, j=GH),
                                 vt[:, par, :, GH * gh:GH * gh + GH, :]).then_inc(stored[par], 16)

            with sp.Fori(0, B) as b:
                for c in range(NC):
                    sp.wait_ge(xn_ready, NC * b + c + 1)
                    sp.dma_start(x[:, c % 2, :, :], x_dram[b, c]).then_inc(x_in[c % 2], 16)
                    if c >= 1:
                        store(b, c - 1)
                store(b, NC - 1)
            for par in range(2):
                sp.wait_ge(stored[par], STORE * (B * NC // 2 + 1))

        @block.gpsimd
        def _(pool):
            for par in range(2):
                pool.memset(vt[:, par, :, :, HD:STRIP], 1.0 if v_ones else 0.0).then_inc(vt_filled, 1)

        @block.vector
        def _(dve):
            dve.sem_inc(xn_ready, 2)
            dve.sem_inc(lo_ready, M)
            dve.sem_inc(v_kept, 1)
            dve.wait_ge(w_in, N_W)
            dve.wait_ge(vt_filled, 2)

            def normalise(b, c):
                G, par = NC * b + c, c % 2
                dve.wait_ge(x_in[par], 16 * (2 * b + c // 2 + 1))
                for t in range(TB):
                    s = dve.bn_stats(stats[:, par, t, :], x[:, par, t, :])
                s.then_inc(chain, 1)
                dve.wait_ge(chain, 4 * G + 1)
                halves_sums(dve, stats[:, par, :, :], mean[:, par, :], half).then_inc(chain, 1)
                dve.wait_ge(chain, 4 * G + 2)
                halves_terms(dve, mean[:, par, :], half).then_inc(chain, 1)
                dve.wait_ge(chain, 4 * G + 3)
                halves_variance(dve, var[:, par, :], half).then_inc(var_ready, 1)
                dve.wait_ge(sd_ready, G + 1)
                dve.reciprocal(rs[:, par, :], sd[:, par, :]).then_inc(chain, 1)
                dve.wait_ge(chain, 4 * G + 4)
                dve.wait_ge(turned, G + 1)
                for t in range(TB):
                    s = dve.tensor_scalar(xn[:, par, t, :], x[:, par, t, :], mean[:, par, t:t + 1],
                                          rs[:, par, t:t + 1], ALU.subtract, ALU.mult)
                s.then_inc(xn_ready, 1)

            def finish(b, c):
                G, par = NC * b + c, c % 2
                dve.wait_ge(stored[par], STORE * (2 * b + c // 2 + 1))
                for m in range(M):
                    dve.wait_ge(hi_ready, M * G + m + 1)
                    dve.scalar_tensor_tensor(out=qk_lo[:, par, m, :], in0=pqk[:, m, :],
                                             scalar=bqk[:, m:m + 1] if biases else 0.0,
                                             in1=qk_hi[:, par, m, :].bitcast(F32), op0=ALU.add,
                                             op1=ALU.subtract).then_inc(lo_ready, 1)
                dve.wait_ge(v_done, G + 3)
                for t in range(TB):
                    src = pv[:, t, :].rearrange("p (h e) -> p h e", e=HD)
                    if biases:
                        s = dve.tensor_tensor(vt[:, par, t, :, 0:HD], src,
                                              bv[:, :].rearrange("p (h e) -> p h e", e=HD), ALU.add)
                    else:
                        s = dve.tensor_copy(vt[:, par, t, :, 0:HD], src)
                s.then_inc(v_kept, 1)

            with dve.Fori(0, B) as b:
                normalise(b, 0)
                for c in range(NC):
                    if c + 1 < NC:
                        normalise(b, c + 1)
                    finish(b, c)

        @block.scalar
        def _(act):
            act.sem_inc(xt_ready, 1)
            act.wait_ge(w_in, N_W)

            def root(b, c):
                G, par = NC * b + c, c % 2
                act.wait_ge(var_ready, G + 1)
                act.activation(sd[:, par, :], var[:, par, :], ACT.Sqrt).then_inc(sd_ready, 1)

            with act.Fori(0, B) as b:
                root(b, 0)
                for c in range(NC):
                    G, par = NC * b + c, c % 2
                    act.wait_ge(turned, G + 3)
                    act.wait_ge(v_done, G + 1)
                    act.activation(xt[:, par, :, :], pt[:, :, :], ACT.Copy).then_inc(xt_ready, 1)
                    if c + 1 < NC:
                        root(b, c + 1)
                    act.wait_ge(stored[par], STORE * (2 * b + c // 2 + 1))
                    for m in range(M):
                        act.wait_ge(qk_done, M * G + m + 1)
                        if biases:
                            act.activation(qk_hi[:, par, m, :], pqk[:, m, :], ACT.Identity,
                                           bias=bqk[:, m:m + 1]).then_inc(hi_ready, 1)
                        else:
                            act.activation(qk_hi[:, par, m, :], pqk[:, m, :], ACT.Copy).then_inc(hi_ready, 1)

        @block.tensor
        def _(pe):
            pe.sem_inc(turned, 2)
            pe.sem_inc(v_done, 2)
            pe.wait_ge(w_in, N_W)

            def turn(b, c):
                G, par = NC * b + c, c % 2
                pe.wait_ge(xn_ready, G + 3)
                pe.wait_ge(xt_ready, G + 1)
                for t in range(TB):
                    for kt in range(KT):
                        mm = pe.transpose(pt[:, kt, t * P:(t + 1) * P], xn[:, par, t, kt * P:(kt + 1) * P],
                                          keep["ident"][:, :])
                mm.then_inc(turned, 1)

            with pe.Fori(0, B) as b:
                turn(b, 0)
                for c in range(NC):
                    G, par = NC * b + c, c % 2
                    pe.wait_ge(xt_ready, G + 2)
                    for m in range(M):
                        pe.wait_ge(lo_ready, M * G + m + 1)
                        for kt in range(KT):
                            mm = pe.matmul(pqk[:, m, :], wqkv[:, kt, m * P:(m + 1) * P], xt[:, par, kt, :],
                                           start=(kt == 0), stop=(kt == KT - 1))
                        mm.then_inc(qk_done, 1)
                        if m == 1 and c + 1 < NC:
                            turn(b, c + 1)
                    pe.wait_ge(v_kept, G + 1)
                    for t in range(TB):
                        for kt in range(KT):
                            mm = pe.matmul(pv[:, t, :], xt[:, par, kt, t * P:(t + 1) * P],
                                           wqkv[:, kt, 2 * D:3 * D], start=(kt == 0), stop=(kt == KT - 1))
                    mm.then_inc(v_done, 1)


E_UNITS = GH * sum(TB * (c + 1) for c in range(NC))
M_UNITS = E_UNITS
KBS = E_UNITS // GH
BAND_UNITS = GH * sum(min(TB * (c + 1), TB + BAND) for c in range(NC))


def attention_plan(with_scores, with_max):
    e, m = [], []
    if with_scores:
        for c in range(NC):
            last = TB * (c + 1) - 1
            for kb in range(last + 1):
                e += [(220.0, ("S", c, kb, j)) for j in range(GH)]
                if kb >= 1:
                    e.append((900.0, ("PV", c, kb - 1)))
                if kb == 1 and c >= 1:
                    e.append((800.0, ("R", c - 1)))
                if kb == 2 and c >= 1:
                    e.append((0.0, ("Y", c - 1)))
            e += [(900.0, ("PV", c, last)), (0.0, ("O", c))]
        e += [(700.0, None), (800.0, ("R", NC - 1)), (700.0, None), (0.0, ("Y", NC - 1))]
    if with_max:
        for c in range(NC):
            units = [("M", c, qb, j, piece) for qb in range(TB) for j in range(GH) for piece in range(c + 1)]
            if c >= 1:
                units[2:2] = [("MT", c - 1)]
                units[5:5] = [("MC", c - 1)]
            m += [(230.0, u) for u in units] + [(0.0, ("MF", c))]
        m += [(230.0, None), (0.0, ("MT", NC - 1)), (230.0, None), (0.0, ("MC", NC - 1))]
    total_e, total_m = sum(x for x, _ in e) or 1.0, sum(x for x, _ in m) or 1.0
    lead = 0.08 if with_scores else 0.0
    timed, at = [], 0.0
    for cost, item in e:
        at += cost
        timed.append((at / total_e, 0, len(timed), item))
    at = 0.0
    for cost, item in m:
        at += cost
        timed.append((lead + (1 - lead) * at / total_m, 1, len(timed), item))
    return one_at_a_time([item for _, _, _, item in sorted(timed) if item])


def one_at_a_time(plan):
    opens, out, held, open_ = {"R": "Y", "MT": "MC"}, [], [], None
    work = list(plan)
    while work or held:
        if open_ is None and held:
            work, held = held + work, []
        item = work.pop(0)
        if item[0] in opens:
            if open_:
                held.append(item)
                continue
            open_ = item
        elif item[0] in ("Y", "MC"):
            if not (open_ and opens[open_[0]] == item[0] and open_[1] == item[1]):
                held.append(item)
                continue
            open_ = None
        out.append(item)
    return out


def attention(nc, name, decayed, keep, dram):
    with ExitStack() as ctx:
        sb = lambda n, s, d: ctx.enter_context(nc.sbuf_tensor(f"{name}_{n}", s, d))
        ps = lambda n, s: ctx.enter_context(nc.psum_tensor(f"{name}_{n}", s, F32))
        sm = phase_semaphores(nc, ctx, name)
        kop = sb("kop", [P, 2, GH, T], F32R)
        qop = sb("qop", [P, 2, GH, T], F32R)
        va = sb("va", [P, 2, BLOCKS, GH, STRIP], F32)
        wt = sb("wt", [P, 2, GH, CH], F32)
        wd = sb("wd", [P, 2, GH, CH], F32) if decayed else None
        mpart = sb("mpart", [P, NC, GH * TB, NC], F32)
        mneg = sb("mneg", [P, NC, GH * TB], F32)
        mrow = sb("mrow", [GH * TB, NC, P], F32R)
        osum = sb("osum", [P, 2, CH], F32)
        y = sb("y", [P, 2, CH], F32)
        pm, pe_, po, px = ps("pm", [P, MBANKS, CH]), ps("ps", [P, EBANKS, CH]), ps("po", [P, CH]), ps("px", [P, CH])

        qk_in = [[sm(f"qk_in{i}{c}") for c in range(NC)] for i in range(2)]
        m_in = [sm(f"m_in{c}") for c in range(NC)]
        v_in, padded, rows_ready = [sm("v_in0"), sm("v_in1")], sm("padded"), sm("rows_ready")
        m_scores, m_reduced, m_final = sm("m_scores"), sm("m_reduced"), sm("m_final")
        x_written, x_read, mrow_ready = sm("x_written"), sm("x_read"), sm("mrow_ready")
        e_scores, e_weights, w_decayed = sm("e_scores"), sm("e_weights"), sm("w_decayed")
        pv_done, o_kept, y_ready = sm("pv_done"), sm("o_kept"), sm("y_ready")
        y_out = [sm(f"y_out{i}") for i in range(2)]
        block = ctx.enter_context(nc.Block())

        qk_g = dram["qk"].rearrange("b g h q (j d) t -> (b g) h q d j t", d=HD)
        v_g = dram["v"].rearrange("b g c p e -> (b g) p c e")
        y_g = dram["y"].rearrange("b g c p t -> (b g) c p t")
        QK_LOADS = 16 * (2 * PAIRS + 1)
        M_DMAS = 16 * GH
        STEP = attention_plan(True, True)
        FIRST = attention_plan(False, True)
        LAST = attention_plan(True, False)

        def x_uses(plan):
            return {item: n for n, item in enumerate(i for i in plan if i[0] in ("R", "MT"))}

        def steps(eng, step):
            step(-1, -1, 1, FIRST, 0)
            with eng.Fori(0, GROUPS // 2 - 1) as i:
                for u in range(2):
                    step(2 * i + u, i, u, STEP, NC + 2 * NC * (2 * i + u))
            step(GROUPS - 2, GROUPS // 2 - 1, 0, STEP, NC + 2 * NC * (GROUPS - 2))
            step(GROUPS - 1, GROUPS // 2 - 1, 1, LAST, NC + 2 * NC * (GROUPS - 1))

        @block.sync
        def _(sp):
            for i in range(2):
                sp.sem_inc(y_out[i], 16)
            for c in range(NC):
                sp.sem_inc(m_in[c], M_DMAS)
            sp.wait_ge(padded, 4)

            def load(g, par):
                for c in range(NC):
                    cols = slice(c * CH, (c + 1) * CH)
                    for r in range(PAIRS):
                        rows = slice(r * HD, (r + 1) * HD)
                        sp.dma_start(kop[rows, par, :, cols].bitcast(F32), qk_g[g, r % 2, 1, :, :, cols]).then_inc(qk_in[par][c], 16)
                        sp.dma_start(qop[rows, par, :, cols].bitcast(F32), qk_g[g, r // 2, 0, :, :, cols]).then_inc(qk_in[par][c], 16)
                    sp.dma_start(qop[MROW:MROW + 1, par, :, cols].bitcast(F32), kop[96:97, par, :, cols].bitcast(F32)).then_inc(qk_in[par][c], 16)
                sp.dma_start(va[:, par, :, :, :].rearrange("p (c t) j e -> p c (t j e)", c=NC), v_g[g])\
                  .then_inc(v_in[par], 16)

            def step(g, i, par, plan, x_before):
                for item in plan:
                    if item[0] == "MC":
                        c = item[1]
                        sp.wait_ge(mrow_ready, NC * (g + 1) + c + 1)
                        for j in range(GH):
                            sp.dma_start(qop[MROW:MROW + 1, 1 - par, j, c * CH:(c + 1) * CH].bitcast(F32),
                                         mrow[TB * j:TB * j + TB, c, :].bitcast(F32)).then_inc(m_in[c], 16)
                    if item[0] == "Y":
                        c = item[1]
                        sp.wait_ge(y_ready, NC * g + c + 3)
                        sp.dma_start(y_g[g, c], y[:, c % 2, :]).then_inc(y_out[c % 2], 16)
                if plan is STEP and not (isinstance(g, int) and g == GROUPS - 2):
                    sp.wait_ge(e_scores, E_UNITS * (g + 1))
                    sp.wait_ge(pv_done, KBS * (g + 1) + 2)
                    load(g + 2, par)

            load(0, 0)
            load(1, 1)
            steps(sp, step)
            for i in range(2):
                sp.wait_ge(y_out[i], 16 * (GROUPS * NC // 2 + 1))

        @block.gpsimd
        def _(pool):
            for par in range(2):
                pool.memset(kop[64:P, par, :, :].bitcast(F32), 0.0).then_inc(rows_ready, 1)
                pool.memset(qop[64:P, par, :, :].bitcast(F32), 0.0).then_inc(padded, 1)
            pool.wait_ge(rows_ready, 2)
            for par in range(2):
                pool.memset(kop[MROW:MROW + 1, par, :, :].bitcast(F32), 1.0).then_inc(padded, 1)
            if decayed:
                def step(g, i, par, plan, x_before):
                    seen = done = 0
                    for item in plan:
                        if item[0] != "S":
                            continue
                        _, c, kb, j = item
                        seen += 1
                        if TB * c - kb > BAND:
                            continue
                        kq = (seen - 1) // GH
                        a, z, u = band_columns(c, kb)
                        pool.wait_ge(e_weights, E_UNITS * g + seen + EBANKS)
                        pool.wait_ge(pv_done, KBS * g + kq + 1)
                        pool.tensor_tensor(wd[:, kq % 2, j, a:z], wt[:, kq % 2, j, a:z],
                                           keep["decay"][:, u:u + z - a], ALU.mult).then_inc(w_decayed, 1)
                        done += 1

                steps(pool, step)

        @block.scalar
        def _(act):
            act.sem_inc(e_weights, EBANKS)
            act.sem_inc(o_kept, 1)

            def step(g, i, par, plan, x_before):
                seen = 0
                for item in plan:
                    if item[0] == "S":
                        _, c, kb, j = item
                        a = P * max(0, kb - TB * c)
                        kq = seen // GH
                        act.wait_ge(e_scores, E_UNITS * g + seen + 1)
                        act.wait_ge(pv_done, KBS * g + kq + 1)
                        act.activation(wt[:, kq % 2, j, a:CH], pe_[:, seen % EBANKS, 0:CH - a], ACT.Exp,
                                       scale=SCALE).then_inc(e_weights, 1)
                        seen += 1
                    if item[0] == "O":
                        c = item[1]
                        act.wait_ge(pv_done, KBS * g + seen // GH + 2)
                        act.wait_ge(y_ready, NC * g + c + 1)
                        act.activation(osum[:, c % 2, :], po[:, :], ACT.Copy).then_inc(o_kept, 1)

            steps(act, step)

        @block.vector
        def _(dve):
            dve.sem_inc(m_reduced, MBANKS)
            dve.sem_inc(x_read, 1)
            dve.sem_inc(y_ready, 2)

            def step(g, i, par, plan, x_before):
                seen = 0
                uses = x_uses(plan)
                for item in plan:
                    if item[0] == "M":
                        _, c, qb, j, piece = item
                        w = CH if piece < c else P * (qb + 1)
                        dve.wait_ge(m_scores, M_UNITS * (g + 1) + seen + 1)
                        dve.tensor_reduce(mpart[:, c, TB * j + qb, piece:piece + 1], pm[:, seen % MBANKS, 0:w],
                                          AX.X, ALU.max).then_inc(m_reduced, 1)
                        seen += 1
                    if item[0] == "MF":
                        c = item[1]
                        dve.wait_ge(m_reduced, M_UNITS * (g + 1) + seen + MBANKS)
                        dve.tensor_reduce(mneg[:, c, :], mpart[:, c, :, 0:c + 1], AX.X, ALU.max,
                                          negate=True).then_inc(m_final, 1)
                    if item[0] == "MC":
                        c = item[1]
                        dve.wait_ge(x_written, x_before + uses[("MT", c)] + 1)
                        dve.wait_ge(m_in[c], M_DMAS * (g + 2))
                        dve.tensor_copy(mrow[:, c, :], px[0:GH * TB, 0:P]).then_inc(x_read, 1)
                        dve.wait_ge(x_read, x_before + uses[("MT", c)] + 2)
                        dve.sem_inc(mrow_ready, 1)
                    if item[0] == "Y":
                        c = item[1]
                        dve.wait_ge(x_written, x_before + uses[("R", c)] + 1)
                        dve.wait_ge(y_out[c % 2], 16 * (2 * g + c // 2 + 1))
                        dve.reciprocal(y[:, c % 2, :], px[:, :]).then_inc(x_read, 1)
                        dve.wait_ge(x_read, x_before + uses[("R", c)] + 2)
                        dve.tensor_tensor(y[:, c % 2, :], osum[:, c % 2, :], y[:, c % 2, :], ALU.mult)\
                           .then_inc(y_ready, 1)

            steps(dve, step)

        @block.tensor
        def _(pe):
            pe.sem_inc(pv_done, 2)
            pe.wait_ge(padded, 4)

            def step(g, i, par, plan, x_before):
                e = m = kq = band = 0
                uses = x_uses(plan)
                for item in plan:
                    if item[0] == "M":
                        _, c, qb, j, piece = item
                        if (qb, j, piece) == (0, 0, 0):
                            pe.wait_ge(qk_in[1 - par][c], QK_LOADS * (i + par + 1))
                        w = CH if piece < c else P * (qb + 1)
                        bank = m % MBANKS
                        pe.wait_ge(m_reduced, M_UNITS * (g + 1) + max(m + 1, MBANKS))
                        q0 = c * CH + qb * P
                        mm = pe.matmul(pm[:, bank, 0:w], qop[:, 1 - par, j, q0:q0 + P],
                                       kop[:, 1 - par, j, piece * CH:piece * CH + w], start=True, stop=piece < c)
                        if piece == c:
                            mm = pe.matmul(pm[:, bank, w - P:w], keep["identb"][:, :], keep["mask_q"][:, :],
                                           start=False, stop=True)
                        mm.then_inc(m_scores, 1)
                        m += 1
                    if item[0] == "MT":
                        c = item[1]
                        pe.wait_ge(m_final, NC * (g + 1) + c + 1)
                        pe.wait_ge(x_read, x_before + uses[item] + 1)
                        pe.matmul(px[0:GH * TB, 0:P], mneg[:, c, :], keep["ident"][:, :], start=True, stop=True)\
                          .then_inc(x_written, 1)
                    if item[0] == "S":
                        _, c, kb, j = item
                        if kb == 0 and j == 0:
                            pe.wait_ge(m_in[c], M_DMAS * (g + 2))
                            if c == 0:
                                pe.wait_ge(v_in[par], 16 * (i + 1))
                        a = P * max(0, kb - TB * c)
                        bank = e % EBANKS
                        pe.wait_ge(e_weights, E_UNITS * g + max(e + 1, EBANKS))
                        diagonal = kb >= TB * c
                        mm = pe.matmul(pe_[:, bank, 0:CH - a], kop[:, par, j, kb * P:(kb + 1) * P],
                                       qop[:, par, j, c * CH + a:(c + 1) * CH], start=True, stop=not diagonal)
                        if diagonal:
                            mm = pe.matmul(pe_[:, bank, 0:P], keep["identb"][:, :], keep["mask_k"][:, :],
                                           start=False, stop=True)
                        mm.then_inc(e_scores, 1)
                        e += 1
                    if item[0] == "PV":
                        _, c, kb = item
                        a = P * max(0, kb - TB * c)
                        last = kb == TB * (c + 1) - 1
                        in_band = TB * c - kb <= BAND
                        pe.wait_ge(e_weights, E_UNITS * g + GH * (kq + 1) + EBANKS)
                        if kb == 0:
                            pe.wait_ge(o_kept, NC * g + c + 1)
                        if decayed:
                            for j in range(GH):
                                mm = pe.matmul(po[STRIP * j:STRIP * (j + 1), a:CH], keep["ones_strip"][:, :],
                                               wt[:, kq % 2, j, a:CH], start=(kb == 0), stop=False)
                            if in_band:
                                band += GH
                                pe.wait_ge(w_decayed, BAND_UNITS * g + band)
                                a, z, _ = band_columns(c, kb)
                                for j in range(GH):
                                    mm = pe.matmul(po[STRIP * j:STRIP * (j + 1), a:z], va[:, par, kb, j, :],
                                                   wd[:, kq % 2, j, a:z], start=False, stop=last)
                        else:
                            for j in range(GH):
                                mm = pe.matmul(po[STRIP * j:STRIP * (j + 1), a:CH], va[:, par, kb, j, :],
                                               wt[:, kq % 2, j, a:CH], start=(kb == 0), stop=last)
                        mm.then_inc(pv_done, 1)
                        kq += 1
                    if item[0] == "R":
                        c = item[1]
                        pe.wait_ge(o_kept, NC * g + c + 2)
                        pe.wait_ge(x_read, x_before + uses[item] + 1)
                        pe.matmul(px[:, :], keep["spread"][:, :], osum[:, c % 2, :], start=True, stop=True)\
                          .then_inc(x_written, 1)

            steps(pe, step)


def band_columns(c, kb):
    a = P * max(0, kb - TB * c)
    z = min(CH, P * (kb - TB * c + BAND + 1))
    return a, z, P * (TB * c - kb) + a


def output_projection(nc, name, x_src, x_dst, xn_dst, w, norm, keep, dram):
    with ExitStack() as ctx:
        sb = lambda n, s, d: ctx.enter_context(nc.sbuf_tensor(f"{name}_{n}", s, d))
        sm = phase_semaphores(nc, ctx, name)
        wp = sb("wp", [P, NG, D], F32)
        bo, gamma, beta = sb("bo", [P, D], F32), sb("gamma", [P, D], F32), sb("beta", [P, D], F32)
        y = sb("y", [P, 2, NG, CH], F32)
        x = sb("x", [P, 2, TB, D], F32)
        xb = sb("xb", [P, 2, TB, D], F32)
        z = sb("z", [P, 2, TB, D], F32)
        zg = sb("zg", [P, 2, TB, D], F32)
        xo = sb("xo", [P, 2, TB, D], F32)
        xn = sb("xn", [P, 2, TB, D], F32)
        stats = sb("stats", [P, TB, 6], F32)
        mean, half = sb("mean", [P, 2, TB], F32), sb("half", [P, 2, TB], F32)
        var, sd, rs = (sb(n, [P, 2, TB], F32) for n in ("var", "sd", "rs"))
        pp = ctx.enter_context(nc.psum_tensor(f"{name}_pp", [P, 2, TB, D], F32))
        zeroed, w_in = sm("zeroed"), sm("w_in")
        y_in, x_in = ([sm(f"{n}{i}") for i in range(2)] for n in ("y_in", "x_in"))
        projected, p_read, chain = sm("projected"), sm("p_read"), sm("chain")
        var_ready, sd_ready, xb_ready = sm("var_ready"), sm("sd_ready"), sm("xb_ready")
        xo_ready, xn_ready = sm("xo_ready"), sm("xn_ready")
        stored = [sm(f"stored{i}") for i in range(2)]
        block = ctx.enter_context(nc.Block())
        NW = 16 * (GH + 3 * bool(norm))
        NORMS = 2 if norm else 1
        LINKS = 4 * NORMS + bool(norm)

        @block.sync
        def _(sp):
            sp.wait_ge(zeroed, 1)
            for j in range(GH):
                sp.dma_start(wp[STRIP * j:STRIP * j + HD, :, :],
                             w.rearrange("(g j d) n -> j d g n", j=GH, d=HD)[j]).then_inc(w_in, 16)
            if norm:
                for t, src in zip((bo, gamma, beta), norm):
                    sp.dma_start(t[:, :], row_of(src).to_broadcast([P, D])).then_inc(w_in, 16)
            for par in range(2):
                sp.sem_inc(stored[par], 32)

            def store(b, c):
                G, par = NC * b + c, c % 2
                sp.wait_ge(xo_ready, G + 3)
                sp.dma_start(x_dst[b, c], xo[:, par, :, :]).then_inc(stored[par], 16)
                sp.wait_ge(xn_ready, G + 1)
                sp.dma_start(xn_dst[b, c], xn[:, par, :, :]).then_inc(stored[par], 16)

            with sp.Fori(0, B) as b:
                for c in range(NC):
                    G, par = NC * b + c, c % 2
                    sp.wait_ge(projected, G + 1)
                    sp.dma_start(y[:, par, :, :], dram["y"][b, :, c].rearrange("g p t -> p g t")).then_inc(y_in[par], 16)
                    sp.wait_ge(xo_ready, G + 1)
                    sp.dma_start(x[:, par, :, :], x_src[b, c]).then_inc(x_in[par], 16)
                    if c >= 1:
                        store(b, c - 1)
                store(b, NC - 1)
            for par in range(2):
                sp.wait_ge(stored[par], 32 * (B * NC // 2 + 1))

        @block.gpsimd
        def _(pool):
            pool.memset(wp[:, :, :], 0.0).then_inc(zeroed, 1)
            pool.wait_ge(w_in, NW)
            if norm:
                with pool.Fori(0, B) as b:
                    for c in range(NC):
                        G, par = NC * b + c, c % 2
                        pool.wait_ge(x_in[par], 16 * (2 * b + c // 2 + 1))
                        pool.wait_ge(xo_ready, G + 1)
                        for t in range(TB):
                            s = pool.tensor_tensor(xb[:, par, t, :], x[:, par, t, :], beta[:, :], ALU.add)
                        s.then_inc(xb_ready, 1)

        @block.tensor
        def _(pe):
            pe.sem_inc(projected, 2)
            pe.wait_ge(w_in, NW)
            with pe.Fori(0, B) as b:
                for c in range(NC):
                    G, par = NC * b + c, c % 2
                    pe.wait_ge(y_in[par], 16 * (2 * b + c // 2 + 1))
                    pe.wait_ge(p_read if norm else xo_ready, G + 1)
                    for t in range(TB):
                        for g in range(NG):
                            mm = pe.matmul(pp[:, par, t, :], y[:, par, g, t * P:(t + 1) * P], wp[:, g, :],
                                           start=(g == 0), stop=(g == NG - 1))
                    mm.then_inc(projected, 1)

        @block.scalar
        def _(act):
            with act.Fori(0, B) as b:
                for c in range(NC):
                    G, par = NC * b + c, c % 2
                    for n in range(NORMS):
                        act.wait_ge(var_ready, NORMS * G + n + 1)
                        act.activation(sd[:, par, :], var[:, par, :], ACT.Sqrt).then_inc(sd_ready, 1)

        @block.vector
        def _(dve):
            dve.sem_inc(p_read, 2)
            dve.sem_inc(xo_ready, 2)
            dve.wait_ge(w_in, NW)

            def moments(G, par, src, n):
                first = LINKS * G + 5 * n + 1
                for t in range(TB):
                    s = dve.bn_stats(stats[:, t, :], src[:, par, t, :])
                s.then_inc(chain, 1)
                dve.wait_ge(chain, first)
                halves_sums(dve, stats, mean[:, par, :], half).then_inc(chain, 1)
                dve.wait_ge(chain, first + 1)
                halves_terms(dve, mean[:, par, :], half).then_inc(chain, 1)
                dve.wait_ge(chain, first + 2)
                halves_variance(dve, var[:, par, :], half).then_inc(var_ready, 1)
                dve.wait_ge(sd_ready, NORMS * G + n + 1)
                dve.reciprocal(rs[:, par, :], sd[:, par, :]).then_inc(chain, 1)
                dve.wait_ge(chain, first + 3)

            with dve.Fori(0, B) as b:
                for c in range(NC):
                    G, par = NC * b + c, c % 2
                    dve.wait_ge(projected, G + 3)
                    if norm:
                        for t in range(TB):
                            s = dve.tensor_tensor(z[:, par, t, :], pp[:, par, t, :], bo[:, :], ALU.add)
                        s.then_inc(p_read, 1)
                        dve.wait_ge(p_read, G + 3)
                        moments(G, par, z, 0)
                        for t in range(TB):
                            s = dve.scalar_tensor_tensor(out=zg[:, par, t, :], in0=z[:, par, t, :],
                                                         scalar=mean[:, par, t:t + 1], in1=gamma[:, :],
                                                         op0=ALU.subtract, op1=ALU.mult)
                        s.then_inc(chain, 1)
                        dve.wait_ge(chain, LINKS * G + 5)
                        dve.wait_ge(xb_ready, G + 1)
                        dve.wait_ge(stored[par], 32 * (2 * b + c // 2 + 1))
                        for t in range(TB):
                            s = dve.scalar_tensor_tensor(out=xo[:, par, t, :], in0=zg[:, par, t, :],
                                                         scalar=rs[:, par, t:t + 1], in1=xb[:, par, t, :],
                                                         op0=ALU.mult, op1=ALU.add)
                        s.then_inc(xo_ready, 1)
                    else:
                        dve.wait_ge(x_in[par], 16 * (2 * b + c // 2 + 1))
                        dve.wait_ge(stored[par], 32 * (2 * b + c // 2 + 1))
                        for t in range(TB):
                            s = dve.tensor_tensor(xo[:, par, t, :], pp[:, par, t, :], x[:, par, t, :], ALU.add)
                        s.then_inc(xo_ready, 1)
                    dve.wait_ge(xo_ready, G + 3)
                    moments(G, par, xo, NORMS - 1)
                    for t in range(TB):
                        s = dve.tensor_scalar(xn[:, par, t, :], xo[:, par, t, :], mean[:, par, t:t + 1],
                                              rs[:, par, t:t + 1], ALU.subtract, ALU.mult)
                    s.then_inc(xn_ready, 1)


def feed_forward(nc, name, x_src, xn_src, dst, keep):
    with ExitStack() as ctx:
        sb = lambda n, s, d: ctx.enter_context(nc.sbuf_tensor(f"{name}_{n}", s, d))
        ps = lambda n, s: ctx.enter_context(nc.psum_tensor(f"{name}_{n}", s, F32))
        sm = phase_semaphores(nc, ctx, name)
        x = sb("x", [P, 2, TB, D], F32)
        xn = sb("xn", [P, 2, TB, D], F32)
        xt_hi, xt_lo = sb("xt_hi", [P, 2, KT, CH], F32R), sb("xt_lo", [P, 2, KT, CH], F32R)
        g = sb("g", [P, 2, CH], F32)
        g_hi, g_lo = sb("g_hi", [P, 2, CH], F32R), sb("g_lo", [P, 2, CH], F32R)
        o = sb("o", [P, KT, CH], F32)
        xo = sb("xo", [P, 2, TB, D], F32)
        pt, ph, po, pb = ps("pt", [P, KT, CH]), ps("ph", [P, 2, CH]), ps("po", [P, KT, CH]), ps("pb", [P, TB, D])
        xn_in, x_in = ([sm(f"{n}{i}") for i in range(2)] for n in ("xn_in", "x_in"))
        turned, hi_ready, lo_ready = sm("turned"), sm("hi_ready"), sm("lo_ready")
        h_done, g_ready, g_hi_ready, g_lo_ready = sm("h_done"), sm("g_ready"), sm("g_hi_ready"), sm("g_lo_ready")
        g_used, o_kept, back, xo_ready = sm("g_used"), sm("o_kept"), sm("back"), sm("xo_ready")
        stored = [sm(f"stored{i}") for i in range(2)]
        block = ctx.enter_context(nc.Block())

        @block.sync
        def _(sp):
            for par in range(2):
                sp.sem_inc(stored[par], 16)

            def store(b, c):
                sp.wait_ge(xo_ready, NC * b + c + 3)
                sp.dma_start(dst[b, c], xo[:, c % 2, :, :]).then_inc(stored[c % 2], 16)

            with sp.Fori(0, B) as b:
                for c in range(NC):
                    G, par = NC * b + c, c % 2
                    sp.wait_ge(turned, G + 1)
                    sp.dma_start(xn[:, par, :, :], xn_src[b, c]).then_inc(xn_in[par], 16)
                    sp.wait_ge(xo_ready, G + 1)
                    sp.dma_start(x[:, par, :, :], x_src[b, c]).then_inc(x_in[par], 16)
                    if c >= 1:
                        store(b, c - 1)
                store(b, NC - 1)
            for par in range(2):
                sp.wait_ge(stored[par], 16 * (B * NC // 2 + 1))

        @block.tensor
        def _(pe):
            pe.sem_inc(turned, 2)
            pe.sem_inc(g_used, 2)
            pe.sem_inc(back, 1)

            def turn(b, c):
                G, par = NC * b + c, c % 2
                pe.wait_ge(xn_in[par], 16 * (2 * b + c // 2 + 1))
                pe.wait_ge(lo_ready, G + 1)
                for t in range(TB):
                    for kt in range(KT):
                        mm = pe.transpose(pt[:, kt, t * P:(t + 1) * P], xn[:, par, t, kt * P:(kt + 1) * P],
                                          keep["ident"][:, :])
                mm.then_inc(turned, 1)

            def hidden(G, par, h):
                pe.wait_ge(g_ready, HT * G + h + 1)
                n = 0
                for kt in range(KT):
                    for part in (xt_hi, xt_lo):
                        mm = pe.matmul(ph[:, h % 2, :], keep["w1s"][:, kt, h * P:(h + 1) * P], part[:, par, kt, :],
                                       start=(n == 0), stop=(n == 2 * KT - 1))
                        n += 1
                mm.then_inc(h_done, 1)

            def output(G, h):
                pe.wait_ge(g_lo_ready, HT * G + h + 3)
                if h == 0:
                    pe.wait_ge(o_kept, G + 1)
                for part, ready in ((g_hi, g_hi_ready), (g_lo, g_lo_ready)):
                    for kt in range(KT):
                        mm = pe.matmul(po[:, kt, :], keep["w2s"][:, h, kt * P:(kt + 1) * P], part[:, h % 2, :],
                                       start=(h == 0 and part is g_hi), stop=(h == HT - 1 and part is g_lo))
                mm.then_inc(g_used, 1)

            with pe.Fori(0, B) as b:
                turn(b, 0)
                for c in range(NC):
                    G, par = NC * b + c, c % 2
                    pe.wait_ge(hi_ready, G + 1)
                    pe.wait_ge(lo_ready, G + 2)
                    for h in range(HT):
                        hidden(G, par, h)
                        if h >= 1:
                            output(G, h - 1)
                        if h == 4 and c + 1 < NC:
                            turn(b, c + 1)
                    output(G, HT - 1)
                    pe.wait_ge(o_kept, G + 2)
                    pe.wait_ge(xo_ready, G + 2)
                    for t in range(TB):
                        for kt in range(KT):
                            mm = pe.transpose(pb[:, t, kt * P:(kt + 1) * P], o[:, kt, t * P:(t + 1) * P],
                                              keep["ident"][:, :])
                    mm.then_inc(back, 1)

        @block.scalar
        def _(act):
            act.sem_inc(g_ready, 2)
            act.sem_inc(o_kept, 1)
            with act.Fori(0, B) as b:
                for c in range(NC):
                    G, par = NC * b + c, c % 2
                    act.wait_ge(turned, G + 3)
                    act.activation(xt_hi[:, par, :, :], pt[:, :, :], ACT.Copy).then_inc(hi_ready, 1)
                    for h in range(HT):
                        act.wait_ge(h_done, HT * G + h + 1)
                        act.wait_ge(g_lo_ready, HT * G + h + 1)
                        act.activation(g[:, h % 2, :], ph[:, h % 2, :], ACT.Gelu, bias=keep["b1"][:, h:h + 1],
                                       scale=keep["alpha1"][:, h:h + 1]).then_inc(g_ready, 1)
                    act.wait_ge(g_used, HT * G + HT + 2)
                    act.wait_ge(back, G + 1)
                    for kt in range(KT):
                        s = act.activation(o[:, kt, :], po[:, kt, :], ACT.Identity, bias=keep["b2"][:, kt:kt + 1],
                                           scale=keep["alpha2"][:, kt:kt + 1])
                    s.then_inc(o_kept, 1)

        @block.vector
        def _(dve):
            dve.sem_inc(lo_ready, 1)
            dve.sem_inc(g_lo_ready, 2)
            dve.sem_inc(xo_ready, 2)

            def add(b, c):
                G, par = NC * b + c, c % 2
                dve.wait_ge(back, G + 2)
                dve.wait_ge(x_in[par], 16 * (2 * b + c // 2 + 1))
                dve.wait_ge(stored[par], 16 * (2 * b + c // 2 + 1))
                dve.tensor_tensor(xo[:, par, :, :], pb[:, :, :], x[:, par, :, :], ALU.add).then_inc(xo_ready, 1)

            with dve.Fori(0, B) as b:
                for c in range(NC):
                    G, par = NC * b + c, c % 2
                    dve.wait_ge(hi_ready, G + 1)
                    dve.tensor_tensor(xt_lo[:, par, :, :], pt[:, :, :], xt_hi[:, par, :, :].bitcast(F32),
                                      ALU.subtract).then_inc(lo_ready, 1)
                    for h in range(HT):
                        dve.wait_ge(g_ready, HT * G + h + 3)
                        dve.wait_ge(g_used, HT * G + h + 1)
                        dve.tensor_copy(g_hi[:, h % 2, :], g[:, h % 2, :]).then_inc(g_hi_ready, 1)
                        dve.wait_ge(g_hi_ready, HT * G + h + 1)
                        dve.tensor_tensor(g_lo[:, h % 2, :], g[:, h % 2, :], g_hi[:, h % 2, :].bitcast(F32),
                                          ALU.subtract).then_inc(g_lo_ready, 1)
                    add(b, c)


INPUTS = ["L0_attn_a_x", "L0_attn_a_W_attn", "L0_attn_a_W_proj", "L0_attn_b_Wq", "L0_attn_b_bq", "L0_attn_b_Wk",
          "L0_attn_b_bk", "L0_attn_b_Wv", "L0_attn_b_bv", "L0_attn_b_Wo", "L0_attn_b_bo", "L0_attn_b_gamma",
          "L0_attn_b_beta", "L0_ffn_w1", "L0_ffn_b1", "L0_ffn_w2", "L0_ffn_b2"]


def build(nc, t, decay, out):
    def chunks(a):
        return a.rearrange("b (c t p) d -> b c p t d", t=TB, p=P)

    with ExitStack() as ctx:
        def dram(n, shape, dt):
            return nc.dram_tensor(n, shape, dt, kind="Internal").ap()

        def sb(n, shape, dt):
            return ctx.enter_context(nc.sbuf_tensor(n, shape, dt))

        x = [chunks(t["L0_attn_a_x"])] + [chunks(dram(f"x{i}", (B, T, D), F32)) for i in range(1, 4)] + [chunks(out)]
        xn = chunks(dram("xn", (B, T, D), F32))
        scratch = {
            "qk": dram("qk", (B, NG, 2, 2, GH * HD, T), F32),
            "v": dram("v", (B, NG, NC, P, TB * GH * STRIP), F32),
            "y": dram("y", (B, NG, NC, P, CH), F32),
        }
        keep = {
            "ident": sb("ident", [P, P], F32), "identb": sb("identb", [P, P], BF16),
            "mask_q": sb("mask_q", [P, P], BF16), "mask_k": sb("mask_k", [P, P], BF16),
            "spread": sb("spread", [P, P], F32), "ones_strip": sb("ones_strip", [P, STRIP], F32),
            "decay": sb("decay", [P, DECAY_COLS], F32),
            "w1s": sb("w1s", [P, KT, FF], F32R), "w2s": sb("w2s", [P, HT, D], F32R),
            "alpha1": sb("alpha1", [P, HT], F32), "alpha2": sb("alpha2", [P, KT], F32),
            "b1": sb("b1", [P, HT], F32), "b2": sb("b2", [P, KT], F32),
        }
        ffn = {"w1": t["L0_ffn_w1"], "b1": t["L0_ffn_b1"], "w2": t["L0_ffn_w2"], "b2": t["L0_ffn_b2"], "decay": decay}
        setup(nc, ffn, keep)
        projections(nc, "qkv_a", x[0], [(t["L0_attn_a_W_attn"], (0, 3 * D))], None, False, keep, scratch)
        attention(nc, "att_a", True, keep, scratch)
        output_projection(nc, "out_a", x[0], x[1], xn, t["L0_attn_a_W_proj"], None, keep, scratch)
        feed_forward(nc, "ffn_a", x[1], xn, x[2], keep)
        projections(nc, "qkv_b", x[2], [(t[f"L0_attn_b_W{n}"], (i * D, (i + 1) * D)) for i, n in enumerate("qkv")],
                    [t[f"L0_attn_b_b{n}"] for n in "qkv"], True, keep, scratch)
        attention(nc, "att_b", False, keep, scratch)
        output_projection(nc, "out_b", x[2], x[3], xn, t["L0_attn_b_Wo"],
                          [t[f"L0_attn_b_{n}"] for n in ("bo", "gamma", "beta")], keep, scratch)
        feed_forward(nc, "ffn_b", x[3], xn, x[4], keep)


def kernel(**inputs):
    import concourse.bacc as bacc
    from concourse.bass_utils import run_bass_kernel_spmd

    nc = bacc.Bacc("TRN2", target_bir_lowering=False, num_devices=1)
    arrays = {f"in_{n}": np.ascontiguousarray(inputs[n]) for n in INPUTS}
    t = {n: nc.dram_tensor(f"in_{n}", arrays[f"in_{n}"].shape, F32, kind="ExternalInput").ap() for n in INPUTS}
    arrays["decay_table"] = decay_table()
    decay = nc.dram_tensor("decay_table", arrays["decay_table"].shape, F32, kind="ExternalInput").ap()
    out = nc.dram_tensor("out", (B, T, D), F32, kind="ExternalOutput").ap()
    nc.disable_value_cache = True
    build(nc, t, decay, out)
    return run_bass_kernel_spmd(nc, [arrays], core_ids=[0]).results[0]["out"]
```

```python
from contextlib import ExitStack

import numpy as np
import concourse.bass as bass
from concourse import mybir

ALU = mybir.AluOpType
ACT = mybir.ActivationFunctionType
AX = mybir.AxisListType
F32 = mybir.dt.float32
F32R = mybir.dt.float32r
BF16 = mybir.dt.bfloat16

P = 128
B, T, D = 2, 2048, 256
H, HD = 16, 16
FF = 1024
KT = D // P
HT = FF // P
CH = 512
NC = T // CH
TB = CH // P
GH = 4
NG = H // GH
GROUPS = B * NG
STRIP = P // GH
SUMS = H * CH // P
BLOCKS = T // P
SCALE = HD ** -0.5
EPS = 1e-5
MASK = -1e37
PAIRS = 4
MROW = PAIRS * HD
ECHOIC, DECAY_LENGTH = 16, 512
SPAN = DECAY_LENGTH - 1
BAND = SPAN // P + 1
DECAY_COLS = (BAND + 1) * P
LEAD = 0.45
MBANKS, EBANKS = 3, 3
EARLY = 3


def decay_table():
    dl = DECAY_LENGTH - ECHOIC + 1
    nums = np.linspace(0.0, 1.0, dl, dtype=np.float32)
    values = (1.0 - np.power(nums, np.float32(1.0 / np.e))).astype(np.float32)
    values = np.concatenate([np.ones(ECHOIC - 1, np.float32), values])
    lag = np.arange(DECAY_COLS)[None, :] - np.arange(P)[:, None]
    return np.where(lag < 0, 0, values[np.clip(lag, 0, DECAY_LENGTH - 1)]).astype(np.float32)


def row_of(vector):
    return vector.rearrange("(a n) -> a n", a=1)


def columns_of(vector):
    return vector.rearrange("(t p) -> p t", p=P)


def phase_semaphores(nc, ctx, name):
    taken = []

    def give_back():
        nc.clear_and_free_semaphores(taken)
        nc.all_engine_barrier()

    def take(n):
        taken.append(nc.alloc_semaphore(name=f"{name}_{n}"))
        return taken[-1]

    ctx.callback(give_back)
    return take


def sequences(eng, body):
    with eng.Fori(0, B - 1) as b:
        body(b, False)
    body(B - 1, True)


def at(chunks, b, c):
    return chunks[b + c // NC, c % NC]


def setup(nc, io, keep):
    with ExitStack() as ctx:
        sb = lambda n, s, d: ctx.enter_context(nc.sbuf_tensor(n, s, d))
        w1 = sb("w1_rows", [P, HT, D], F32)
        w2 = sb("w2_rows", [P, KT, FF], F32)
        neg = sb("w_negative", [P, HT, D], F32)
        sign1 = sb("w1_sign", [P, HT, D], F32)
        sign2 = sb("w2_sign", [P, KT, FF], F32)
        turned = ctx.enter_context(nc.psum_tensor("w_turned", [P, 4, CH], F32))
        sem = phase_semaphores(nc, ctx, "setup")
        w_loaded, ident_ready, zeroed = sem("w_loaded"), sem("ident_ready"), sem("zeroed")
        sign_step, signs_ready = sem("sign_step"), sem("signs_ready")
        w_turned, w_kept = sem("w_turned_sem"), sem("w_kept")
        const_loaded = sem("const_loaded")
        ident, identr = keep["ident"], keep["identr"]
        block = ctx.enter_context(nc.Block())

        @block.sync
        def _(sp):
            sp.dma_start(w1[:, :, :], io["w1"].rearrange("(t p) d -> p t d", p=P)).then_inc(w_loaded, 16)
            sp.dma_start(w2[:, :, :], io["w2"].rearrange("(t p) d -> p t d", p=P)).then_inc(w_loaded, 16)
            with nc.allow_non_contiguous_dma(reason="biases as columns, once"):
                sp.dma_start(keep["b1"][:, :], columns_of(io["b1"])).then_inc(const_loaded, 16)
                sp.dma_start(keep["b2"][:, :], columns_of(io["b2"])).then_inc(const_loaded, 16)
            sp.dma_start(keep["decay"][:, :], io["decay"]).then_inc(const_loaded, 16)
            sp.wait_ge(const_loaded, 48)

        @block.gpsimd
        def _(pool):
            pool.memset(ident[:, :], 0.0).then_inc(zeroed, 1)
            pool.memset(identr[:, :].bitcast(F32), 0.0).then_inc(zeroed, 1)
            pool.memset(keep["mask_q"][:, :].bitcast(F32), 0.0).then_inc(zeroed, 1)
            pool.memset(keep["mask_k"][:, :].bitcast(F32), 0.0).then_inc(zeroed, 1)
            pool.memset(keep["ones_strip"][:, 0:HD], 0.0).then_inc(zeroed, 1)
            pool.memset(keep["ones_strip"][:, HD:STRIP], 1.0).then_inc(zeroed, 1)
            pool.wait_ge(zeroed, 6)
            for m in (ident, identr):
                pool.affine_select(out=m[:, :], in_=m[:, :].bitcast(F32), compare_op=ALU.not_equal, fill=1.0, base=0,
                                   pattern=[[-1, P]], channel_multiplier=1).then_inc(ident_ready, 1)
            pool.affine_select(out=keep["mask_q"][:, :], in_=keep["mask_q"][:, :].bitcast(F32), compare_op=ALU.is_ge,
                               fill=MASK, base=0, pattern=[[-1, P]], channel_multiplier=1).then_inc(ident_ready, 1)
            pool.affine_select(out=keep["mask_k"][:, :], in_=keep["mask_k"][:, :].bitcast(F32), compare_op=ALU.is_ge,
                               fill=MASK, base=0, pattern=[[1, P]], channel_multiplier=-1).then_inc(ident_ready, 1)

        @block.vector
        def _(dve):
            dve.wait_ge(w_loaded, 32)
            for w, s, n, tiles, alpha in ((w1, sign1, D, HT, keep["alpha1"]), (w2, sign2, FF, KT, keep["alpha2"])):
                step = 4 * (w is w2)
                below = neg[:, :, :].rearrange("p a b -> p (a b)").rearrange("p (t d) -> p t d", t=tiles)
                dve.tensor_reduce(alpha[:, :], w[:, :, :], AX.X, ALU.add,
                                  apply_absolute_value=True).then_inc(sign_step, 1)
                dve.wait_ge(sign_step, step + 1)
                dve.tensor_scalar(alpha[:, :], alpha[:, :], 1.0 / n, None, ALU.mult).then_inc(sign_step, 1)
                dve.wait_ge(sign_step, step + 2)
                dve.tensor_scalar(below, w[:, :, :], 0.0, None, ALU.is_lt).then_inc(sign_step, 1)
                dve.wait_ge(sign_step, step + 3)
                dve.scalar_tensor_tensor(out=s[:, :, :], in0=w[:, :, :], scalar=0.0, in1=below,
                                         op0=ALU.is_gt, op1=ALU.subtract).then_inc(sign_step, 1)
                dve.wait_ge(sign_step, step + 4)
            dve.sem_inc(signs_ready, 1)
            for n in range(8):
                dve.wait_ge(w_turned, n + 1)
                if n < 4:
                    kt, half = n // 2, n % 2
                    dst = keep["w1s"][:, kt, half * CH:(half + 1) * CH]
                    dve.tensor_copy(dst, turned[:, n % 4, :]).then_inc(w_kept, 1)
                else:
                    ht = 2 * (n - 4)
                    dst = keep["w2s"][:, ht:ht + 2, :]
                    dve.tensor_copy(dst, turned[:, n % 4, :].rearrange("p (a d) -> p a d", a=2)).then_inc(w_kept, 1)

        @block.tensor
        def _(pe):
            pe.wait_ge(ident_ready, 1)
            pe.wait_ge(signs_ready, 1)
            for n in range(8):
                if n >= 4:
                    pe.wait_ge(w_kept, n - 3)
                for q in range(4):
                    if n < 4:
                        kt, half = n // 2, n % 2
                        src = sign1[:, 4 * half + q, kt * P:(kt + 1) * P]
                    else:
                        ht = 2 * (n - 4) + q // 2
                        src = sign2[:, q % 2, ht * P:(ht + 1) * P]
                    mm = pe.transpose(turned[:, n % 4, q * P:(q + 1) * P], src, ident[:, :])
                mm.then_inc(w_turned, 1)


def halves_sums(dve, stats, mean, half):
    dve.tensor_tensor(mean, stats[:, :, 1], stats[:, :, 4], ALU.add)
    dve.tensor_tensor(half[:, 0, :], stats[:, :, 1], stats[:, :, 4], ALU.subtract)
    return dve.tensor_tensor(half[:, 1, :], stats[:, :, 2], stats[:, :, 5], ALU.add)


def halves_terms(dve, mean, half):
    dve.tensor_scalar(mean, mean, 0.5, None, ALU.mult)
    dve.tensor_tensor(half[:, 0, :], half[:, 0, :], half[:, 0, :], ALU.mult)
    return dve.tensor_scalar(half[:, 1, :], half[:, 1, :], 1.0 / D, EPS, ALU.mult, ALU.add)


def halves_variance(dve, var, half):
    return dve.scalar_tensor_tensor(out=var, in0=half[:, 0, :], scalar=0.25, in1=half[:, 1, :],
                                    op0=ALU.mult, op1=ALU.add)


def projections(nc, name, x_dram, weights, biases, v_ones, keep, dram):
    with ExitStack() as ctx:
        sb = lambda n, s, d: ctx.enter_context(nc.sbuf_tensor(f"{name}_{n}", s, d))
        ps = lambda n, s: ctx.enter_context(nc.psum_tensor(f"{name}_{n}", s, F32))
        sm = phase_semaphores(nc, ctx, name)
        wqkv = sb("wqkv", [P, KT, 3 * D], F32)
        bqk = sb("bqk", [P, 2 * KT], F32)
        bv = sb("bv", [P, D], F32)
        x = sb("x", [P, 2, TB, D], F32)
        xn = sb("xn", [P, 2, TB, D], F32)
        xt = sb("xt", [P, 2, KT, CH], F32)
        stats = sb("stats", [P, 2, TB, 6], F32)
        mean, half = sb("mean", [P, 2, TB], F32), sb("half", [P, 2, TB], F32)
        var = sb("var", [P, 2, TB], F32)
        sd = sb("sd", [P, 2, TB], F32)
        rs = sb("rs", [P, 2, TB], F32)
        qk_hi = sb("qk_hi", [P, 2, 2 * KT, CH], F32R)
        qk_lo = sb("qk_lo", [P, 2, 2 * KT, CH], F32R)
        vt = sb("vt", [P, 2, TB, H, STRIP], F32)
        pt = ps("pt", [P, KT, CH])
        pqk = ps("pqk", [P, 2 * KT, CH])
        pv = ps("pv", [P, TB, D])
        w_in, x_in, chain = sm("w_in"), [sm("x_in0"), sm("x_in1")], sm("chain")
        var_ready, sd_ready, xn_ready = sm("var_ready"), sm("sd_ready"), sm("xn_ready")
        turned, xt_ready, qk_done, v_done = sm("turned"), sm("xt_ready"), sm("qk_done"), sm("v_done")
        hi_ready, lo_ready, v_kept, vt_filled = sm("hi_ready"), sm("lo_ready"), sm("v_kept"), sm("vt_filled")
        stored = [sm(f"stored{i}") for i in range(2)]
        block = ctx.enter_context(nc.Block())
        M = 2 * KT
        STORE = 16 * (8 + NG)
        N_W = 16 * (len(weights) + 3 * bool(biases))

        @block.sync
        def _(sp):
            def load(b, c):
                sp.wait_ge(xn_ready, NC * b + c + 1)
                sp.dma_start(x[:, c % 2, :, :], at(x_dram, b, c)).then_inc(x_in[c % 2], 16)

            load(0, 0)
            for src, (a, z) in weights:
                sp.dma_start(wqkv[:, :, a:z], src.rearrange("(t p) n -> p t n", p=P)).then_inc(w_in, 16)
            if biases:
                with nc.allow_non_contiguous_dma(reason="biases as columns, once"):
                    sp.dma_start(bqk[:, 0:KT], columns_of(biases[0])).then_inc(w_in, 16)
                    sp.dma_start(bqk[:, KT:M], columns_of(biases[1])).then_inc(w_in, 16)
                sp.dma_start(bv[:, :], row_of(biases[2]).to_broadcast([P, D])).then_inc(w_in, 16)
            for par in range(2):
                sp.sem_inc(stored[par], STORE)

            def store(b, c):
                G, par = NC * b + c, c % 2
                sp.wait_ge(hi_ready, M * G + M)
                sp.wait_ge(lo_ready, M * G + 2 * M)
                for hl, t in ((0, qk_hi), (1, qk_lo)):
                    for a in range(2):
                        for qk in range(2):
                            dst = dram["qk"][b, :, hl, qk, :, c * CH:(c + 1) * CH]
                            dst = dst.rearrange("(m a) p t -> a p m t", a=2)[a]
                            sp.dma_start(dst, t[64 * a:64 * a + 64, par, KT * qk:KT * qk + KT, :].bitcast(F32))\
                              .then_inc(stored[par], 16)
                sp.wait_ge(v_kept, G + 2)
                for gh in range(NG):
                    sp.dma_start(dram["v"][b, gh, c].rearrange("p (t j e) -> p t j e", t=TB, j=GH),
                                 vt[:, par, :, GH * gh:GH * gh + GH, :]).then_inc(stored[par], 16)

            load(0, 1)

            def body(b, last):
                for c in range(NC):
                    if not last or c + 2 < NC:
                        load(b, c + 2)
                    store(b, c)

            sequences(sp, body)
            for par in range(2):
                sp.wait_ge(stored[par], STORE * (B * NC // 2 + 1))

        @block.gpsimd
        def _(pool):
            for par in range(2):
                pool.memset(vt[:, par, :, :, HD:STRIP], 1.0 if v_ones else 0.0).then_inc(vt_filled, 1)

        @block.vector
        def _(dve):
            dve.sem_inc(xn_ready, 2)
            dve.sem_inc(lo_ready, M)
            dve.sem_inc(v_kept, 1)

            def normalise(b, c):
                G, par = NC * b + c, c % 2
                dve.wait_ge(x_in[par], 16 * (2 * b + c // 2 + 1))
                for t in range(TB):
                    s = dve.bn_stats(stats[:, par, t, :], x[:, par, t, :])
                s.then_inc(chain, 1)
                dve.wait_ge(chain, 4 * G + 1)
                halves_sums(dve, stats[:, par, :, :], mean[:, par, :], half).then_inc(chain, 1)
                dve.wait_ge(chain, 4 * G + 2)
                halves_terms(dve, mean[:, par, :], half).then_inc(chain, 1)
                dve.wait_ge(chain, 4 * G + 3)
                halves_variance(dve, var[:, par, :], half).then_inc(var_ready, 1)
                dve.wait_ge(sd_ready, G + 1)
                dve.reciprocal(rs[:, par, :], sd[:, par, :]).then_inc(chain, 1)
                dve.wait_ge(chain, 4 * G + 4)
                dve.wait_ge(turned, G + 1)
                for t in range(TB):
                    s = dve.tensor_scalar(xn[:, par, t, :], x[:, par, t, :], mean[:, par, t:t + 1],
                                          rs[:, par, t:t + 1], ALU.subtract, ALU.mult)
                s.then_inc(xn_ready, 1)

            def finish(b, c):
                G, par = NC * b + c, c % 2
                dve.wait_ge(stored[par], STORE * (2 * b + c // 2 + 1))
                for m in range(M):
                    dve.wait_ge(hi_ready, M * G + m + 1)
                    dve.scalar_tensor_tensor(out=qk_lo[:, par, m, :], in0=pqk[:, m, :],
                                             scalar=bqk[:, m:m + 1] if biases else 0.0,
                                             in1=qk_hi[:, par, m, :].bitcast(F32), op0=ALU.add,
                                             op1=ALU.subtract).then_inc(lo_ready, 1)
                dve.wait_ge(v_done, G + 3)
                for t in range(TB):
                    src = pv[:, t, :].rearrange("p (h e) -> p h e", e=HD)
                    if biases:
                        s = dve.tensor_tensor(vt[:, par, t, :, 0:HD], src,
                                              bv[:, :].rearrange("p (h e) -> p h e", e=HD), ALU.add)
                    else:
                        s = dve.tensor_copy(vt[:, par, t, :, 0:HD], src)
                s.then_inc(v_kept, 1)

            def body(b, last):
                for c in range(NC):
                    if not last or c + 1 < NC:
                        normalise(b, c + 1)
                    finish(b, c)

            normalise(0, 0)
            dve.wait_ge(w_in, N_W)
            dve.wait_ge(vt_filled, 2)
            sequences(dve, body)

        @block.scalar
        def _(act):
            act.sem_inc(xt_ready, 1)

            def root(b, c):
                G, par = NC * b + c, c % 2
                act.wait_ge(var_ready, G + 1)
                act.activation(sd[:, par, :], var[:, par, :], ACT.Sqrt).then_inc(sd_ready, 1)

            def body(b, last):
                for c in range(NC):
                    G, par = NC * b + c, c % 2
                    act.wait_ge(turned, G + 3)
                    act.wait_ge(v_done, G + 1)
                    act.activation(xt[:, par, :, :], pt[:, :, :], ACT.Copy).then_inc(xt_ready, 1)
                    if not last or c + 1 < NC:
                        root(b, c + 1)
                    act.wait_ge(stored[par], STORE * (2 * b + c // 2 + 1))
                    for m in range(M):
                        act.wait_ge(qk_done, M * G + m + 1)
                        if biases:
                            act.activation(qk_hi[:, par, m, :], pqk[:, m, :], ACT.Identity,
                                           bias=bqk[:, m:m + 1]).then_inc(hi_ready, 1)
                        else:
                            act.activation(qk_hi[:, par, m, :], pqk[:, m, :], ACT.Copy).then_inc(hi_ready, 1)

            root(0, 0)
            act.wait_ge(w_in, N_W)
            sequences(act, body)

        @block.tensor
        def _(pe):
            pe.sem_inc(turned, 2)
            pe.sem_inc(v_done, 2)

            def turn(b, c):
                G, par = NC * b + c, c % 2
                pe.wait_ge(xn_ready, G + 3)
                pe.wait_ge(xt_ready, G + 1)
                for t in range(TB):
                    for kt in range(KT):
                        mm = pe.transpose(pt[:, kt, t * P:(t + 1) * P], xn[:, par, t, kt * P:(kt + 1) * P],
                                          keep["ident"][:, :])
                mm.then_inc(turned, 1)

            def body(b, last):
                for c in range(NC):
                    G, par = NC * b + c, c % 2
                    pe.wait_ge(xt_ready, G + 2)
                    for m in range(M):
                        pe.wait_ge(lo_ready, M * G + m + 1)
                        for kt in range(KT):
                            mm = pe.matmul(pqk[:, m, :], wqkv[:, kt, m * P:(m + 1) * P], xt[:, par, kt, :],
                                           start=(kt == 0), stop=(kt == KT - 1))
                        mm.then_inc(qk_done, 1)
                        if m == 2 and (not last or c + 1 < NC):
                            turn(b, c + 1)
                    pe.wait_ge(v_kept, G + 1)
                    for t in range(TB):
                        for kt in range(KT):
                            mm = pe.matmul(pv[:, t, :], xt[:, par, kt, t * P:(t + 1) * P],
                                           wqkv[:, kt, 2 * D:3 * D], start=(kt == 0), stop=(kt == KT - 1))
                    mm.then_inc(v_done, 1)

            turn(0, 0)
            pe.wait_ge(w_in, N_W)
            sequences(pe, body)


E_UNITS = GH * sum(TB * (c + 1) for c in range(NC))
M_UNITS = E_UNITS
KBS = E_UNITS // GH
BAND_UNITS = GH * sum(min(TB * (c + 1), TB + BAND) for c in range(NC))


def attention_plan(weights, rest, ahead, together):
    e, m, waiting, leaving = [], [], [], None
    for c in range(NC):
        last = TB * (c + 1) - 1
        for kb in range(last + 1):
            for j in range(GH):
                e.append((60.0 + CH - P * max(0, kb - TB * c), ("S", c, kb, j)))
                if leaving is not None and j == 1:
                    e.append((0.0, ("O", leaving)))
                    leaving = None
            if len(waiting) == together:
                e += [(0.0, item) for item in waiting]
                leaving = waiting[-1][1] if waiting[-1][2] == TB * (waiting[-1][1] + 1) - 1 else None
                waiting = []
            waiting.append(("PV", c, kb))
    e += [(0.0, item) for item in waiting] + [(0.0, ("O", NC - 1))]
    n = 0
    for c in range(NC):
        units = []
        for qb in range(TB):
            for j in range(GH):
                for piece in range(c + 1):
                    units.append((60.0 + (CH if piece < c else P * (qb + 1)), ("M", n, c, qb, j, piece)))
                    n += 1
        m += units + [(0.0, ("MF", c)), (400.0, ("MT", c)), (400.0, ("MC", c))]
    m = spaced(m)
    total_e, total_m = sum(x for x, _ in e), sum(x for x, _ in m)
    timed, at = [], 0.0
    for cost, item in e if weights else ():
        at += cost
        timed.append((at / total_e, 0, len(timed), item))
    at = 0.0
    for cost, item in m:
        at += cost
        t = at / total_m - LEAD
        if t < 0 and ahead:
            timed.append((1 + t, 2, len(timed), (item[0], 1, *item[1:])))
        if t >= 0 and rest:
            timed.append((t, 1, len(timed), (item[0], 0, *item[1:])))
    return [item for _, _, _, item in sorted(timed)]


def spaced(m):
    out, late = [], []
    for cost, item in m:
        if item[0] in ("MT", "MC"):
            late.append([3 if item[0] == "MT" else 6, item])
            continue
        out.append((cost, item))
        for x in late:
            x[0] -= 1
        out += [(0.0, x[1]) for x in late if x[0] == 0]
        late = [x for x in late if x[0] > 0]
    for x in late:
        out += [(400.0, x[1])]
    return out


def attention(nc, name, decayed, keep, dram):
    with ExitStack() as ctx:
        sb = lambda n, s, d: ctx.enter_context(nc.sbuf_tensor(f"{name}_{n}", s, d))
        ps = lambda n, s: ctx.enter_context(nc.psum_tensor(f"{name}_{n}", s, F32))
        sm = phase_semaphores(nc, ctx, name)
        kop = sb("kop", [P, 2, GH, T], F32R)
        qop = sb("qop", [P, 2, GH, T], F32R)
        va = sb("va", [P, 2, BLOCKS, GH, STRIP], F32)
        buffers, together = (2, 1) if decayed else (4, 1)
        wt = sb("wt", [P, buffers, GH, CH], F32)
        wd = sb("wd", [P, 2, GH, CH], F32) if decayed else None
        mpart = sb("mpart", [P, NC, GH * TB, NC], F32)
        mneg = sb("mneg", [P, NC, GH * TB], F32)
        mrow = sb("mrow", [GH * TB, NC, P], F32R)
        y = sb("y", [P, 2, CH], F32)
        pm, pe_, po, px = ps("pm", [P, MBANKS, CH]), ps("ps", [P, EBANKS, CH]), ps("po", [P, CH]), ps("px", [P, CH])

        qk_in = [[sm(f"qk_in{i}{c}") for c in range(NC)] for i in range(2)]
        m_in = [sm(f"m_in{c}") for c in range(NC)]
        v_in = [sm("v_in0"), sm("v_in1")]
        q_padded, k_padded = ([sm(f"{n}{i}") for i in range(2)] for n in ("q_padded", "k_padded"))
        m_scores, m_reduced, m_final = sm("m_scores"), sm("m_reduced"), sm("m_final")
        x_written, x_read, mrow_ready = sm("x_written"), sm("x_read"), sm("mrow_ready")
        e_scores, e_weights, w_decayed = sm("e_scores"), sm("e_weights"), sm("w_decayed")
        w_masked, w_turn = sm("w_masked"), sm("w_turn")
        pv_done, o_kept = sm("pv_done"), sm("o_kept")
        y_out = [sm(f"y_out{i}") for i in range(2)]
        block = ctx.enter_context(nc.Block())

        qk_g = dram["qk"].rearrange("b g h q (j d) t -> (b g) h q d j t", d=HD)
        v_g = dram["v"].rearrange("b g c p e -> (b g) p c e")
        y_g = dram["y"].rearrange("b g c p t -> (b g) c p t")
        QK_LOADS = 16 * (2 * PAIRS + 1)
        M_DMAS = 16 * GH
        STEP = attention_plan(True, True, True, together)
        FIRST = attention_plan(False, False, True, together)
        LAST = attention_plan(True, True, False, together)
        AHEAD = sum(item[0] == "MT" for item in FIRST)

        def steps(eng, step):
            step(-1, -1, 1, FIRST)
            with eng.Fori(0, GROUPS // 2 - 1) as i:
                for u in range(2):
                    step(2 * i + u, i, u, STEP)
            step(GROUPS - 2, GROUPS // 2 - 1, 0, STEP)
            step(GROUPS - 1, GROUPS // 2 - 1, 1, LAST)

        def pad(eng, t, par, padded):
            for c in range(NC):
                eng.memset(t[MROW:P, par, :, c * CH:(c + 1) * CH].bitcast(F32), 1.0 if t is kop else 0.0)\
                   .then_inc(padded, 1)

        def maxima(g, i, par, d):
            return (par, i) if d == 0 else (1 - par, i + par)

        @block.sync
        def _(sp):
            for i in range(2):
                sp.sem_inc(y_out[i], 16)
            for c in range(NC):
                sp.sem_inc(m_in[c], M_DMAS)

            def load(g, par, first):
                for c in range(NC):
                    cols = slice(c * CH, (c + 1) * CH)
                    for r in range(PAIRS):
                        rows = slice(r * HD, (r + 1) * HD)
                        sp.dma_start(kop[rows, par, :, cols].bitcast(F32), qk_g[g, r % 2, 1, :, :, cols]).then_inc(qk_in[par][c], 16)
                        sp.dma_start(qop[rows, par, :, cols].bitcast(F32), qk_g[g, r // 2, 0, :, :, cols]).then_inc(qk_in[par][c], 16)
                    if first:
                        sp.wait_ge(q_padded[par], c + 1)
                    sp.dma_start(qop[MROW:MROW + 1, par, :, cols].bitcast(F32),
                                 qop[96:97, par, :, cols].bitcast(F32)).then_inc(qk_in[par][c], 16)
                sp.dma_start(va[:, par, :, :, :].rearrange("p (c t) j e -> p c (t j e)", c=NC), v_g[g])\
                  .then_inc(v_in[par], 16)

            def step(g, i, par, plan):
                for item in plan:
                    if item[0] == "MC":
                        _, d, c = item
                        mpar, _ = maxima(g, i, par, d)
                        sp.wait_ge(x_read, NC * (g + d) + c + 2)
                        for j in range(GH):
                            sp.dma_start(qop[MROW:MROW + 1, mpar, j, c * CH:(c + 1) * CH].bitcast(F32),
                                         mrow[TB * j:TB * j + TB, c, :].bitcast(F32)).then_inc(m_in[c], 16)
                    if item[0] == "O":
                        c = item[1]
                        sp.wait_ge(o_kept, NC * g + c + 2)
                        sp.dma_start(y_g[g, c], y[:, c % 2, :]).then_inc(y_out[c % 2], 16)
                if plan is STEP and not (isinstance(g, int) and g == GROUPS - 2):
                    sp.wait_ge(e_scores, E_UNITS * (g + 1))
                    sp.wait_ge(pv_done, KBS * (g + 1) + buffers)
                    load(g + 2, par, False)

            load(0, 0, True)
            load(1, 1, True)
            steps(sp, step)
            for i in range(2):
                sp.wait_ge(y_out[i], 16 * (GROUPS * NC // 2 + 1))

        @block.gpsimd
        def _(pool):
            for t, par, padded in ((kop, 0, k_padded), (qop, 1, q_padded), (kop, 1, k_padded)):
                pad(pool, t, par, padded[par])
            pool.wait_ge(k_padded[1], NC)
            if decayed:
                def step(g, i, par, plan):
                    seen = done = 0
                    for item in plan:
                        if item[0] != "S":
                            continue
                        _, c, kb, j = item
                        seen += 1
                        if TB * c - kb > BAND:
                            continue
                        kq = (seen - 1) // GH
                        a, z, u = band_columns(c, kb)
                        pool.wait_ge(e_weights, E_UNITS * g + seen + EBANKS)
                        pool.wait_ge(pv_done, KBS * g + kq + 1)
                        pool.tensor_tensor(wd[:, kq % 2, j, a:z], wt[:, kq % 2, j, a:z],
                                           keep["decay"][:, u:u + z - a], ALU.mult).then_inc(w_decayed, 1)
                        done += 1

                steps(pool, step)
            else:
                def step(g, i, par, plan):
                    seen = 0
                    for item in plan:
                        if item[0] != "S":
                            continue
                        _, c, kb, j = item
                        seen += 1
                        if kb < TB * c or j < GH - 1:
                            continue
                        pool.wait_ge(e_weights, E_UNITS * g + seen + EBANKS)
                        pool.sem_inc(w_turn, 1)
                        block = wt[:, (seen // GH - 1) % buffers, :, P * (kb - TB * c):P * (kb - TB * c + 1)]
                        pool.affine_select(out=block, in_=block, compare_op=ALU.is_ge, fill=0.0, base=0,
                                           pattern=[[0, GH], [1, P]], channel_multiplier=-1).then_inc(w_masked, 1)

                steps(pool, step)

        @block.scalar
        def _(act):
            act.sem_inc(e_weights, EBANKS)
            act.sem_inc(o_kept, 1)

            def step(g, i, par, plan):
                seen = 0
                for item in plan:
                    if item[0] == "S":
                        _, c, kb, j = item
                        a = P * max(0, kb - TB * c)
                        kq = seen // GH
                        act.wait_ge(e_scores, E_UNITS * g + seen + 1)
                        act.wait_ge(pv_done, KBS * g + kq + 1)
                        act.activation(wt[:, kq % buffers, j, a:CH], pe_[:, seen % EBANKS, 0:CH - a], ACT.Exp,
                                       scale=SCALE).then_inc(e_weights, 1)
                        seen += 1
                    if item[0] == "O":
                        c = item[1]
                        act.wait_ge(pv_done, KBS * g + TB * (c + 1) * (c + 2) // 2 + buffers)
                        act.wait_ge(y_out[c % 2], 16 * (2 * g + c // 2 + 1))
                        act.activation(y[:, c % 2, :], po[:, :], ACT.Copy).then_inc(o_kept, 1)

            steps(act, step)

        @block.vector
        def _(dve):
            pad(dve, qop, 0, q_padded[0])
            dve.sem_inc(m_reduced, MBANKS)
            dve.sem_inc(x_read, 1)

            def step(g, i, par, plan):
                for item in plan:
                    if item[0] == "M":
                        _, d, n, c, qb, j, piece = item
                        w = CH if piece < c else P * (qb + 1)
                        dve.wait_ge(m_scores, M_UNITS * (g + d) + n + 1)
                        dve.tensor_reduce(mpart[:, c, TB * j + qb, piece:piece + 1], pm[:, n % MBANKS, 0:w],
                                          AX.X, ALU.max).then_inc(m_reduced, 1)
                    if item[0] == "MF":
                        _, d, c = item
                        dve.wait_ge(m_reduced, M_UNITS * (g + d) + GH * sum(TB * (a + 1) for a in range(c + 1)) + MBANKS)
                        dve.tensor_reduce(mneg[:, c, :], mpart[:, c, :, 0:c + 1], AX.X, ALU.max,
                                          negate=True).then_inc(m_final, 1)
                    if item[0] == "MC":
                        _, d, c = item
                        dve.wait_ge(x_written, NC * (g + d) + c + 1)
                        dve.wait_ge(m_in[c], M_DMAS * (g + d + 1))
                        dve.tensor_copy(mrow[:, c, :], px[0:GH * TB, 0:P]).then_inc(x_read, 1)

            steps(dve, step)

        @block.tensor
        def _(pe):
            pe.sem_inc(pv_done, buffers)
            def step(g, i, par, plan):
                e = kq = band = masked = 0
                for item in plan:
                    if item[0] == "M":
                        _, d, n, c, qb, j, piece = item
                        mpar, before = maxima(g, i, par, d)
                        if (qb, j, piece) == (0, 0, 0):
                            if plan is FIRST:
                                pe.wait_ge(k_padded[0], c + 1)
                                pe.wait_ge(q_padded[0], c + 1)
                            elif plan is STEP and d == 1 and par == 0:
                                pe.wait_ge(k_padded[1], c + 1)
                                pe.wait_ge(q_padded[1], c + 1)
                            pe.wait_ge(qk_in[mpar][c], QK_LOADS * (before + 1))
                        w = CH if piece < c else P * (qb + 1)
                        bank = n % MBANKS
                        pe.wait_ge(m_reduced, M_UNITS * (g + d) + max(n + 1, MBANKS))
                        q0 = c * CH + qb * P
                        mm = pe.matmul(pm[:, bank, 0:w], qop[:, mpar, j, q0:q0 + P],
                                       kop[:, mpar, j, piece * CH:piece * CH + w], start=True, stop=piece < c)
                        if piece == c:
                            mm = pe.matmul(pm[:, bank, w - P:w], keep["identr"][:, :], keep["mask_q"][:, :],
                                           start=False, stop=True)
                        mm.then_inc(m_scores, 1)
                    if item[0] == "MT":
                        _, d, c = item
                        pe.wait_ge(m_final, NC * (g + d) + c + 1)
                        pe.wait_ge(x_read, NC * (g + d) + c + 1)
                        pe.matmul(px[0:GH * TB, 0:P], mneg[:, c, :], keep["ident"][:, :], start=True, stop=True)\
                          .then_inc(x_written, 1)
                    if item[0] == "S":
                        _, c, kb, j = item
                        if kb == 0 and j == 0:
                            pe.wait_ge(m_in[c], M_DMAS * (g + 2))
                            if c == 0:
                                pe.wait_ge(v_in[par], 16 * (i + 1))
                        a = P * max(0, kb - TB * c)
                        bank = e % EBANKS
                        pe.wait_ge(e_weights, E_UNITS * g + max(e + 1, EBANKS))
                        diagonal = decayed and kb >= TB * c
                        mm = pe.matmul(pe_[:, bank, 0:CH - a], kop[:, par, j, kb * P:(kb + 1) * P],
                                       qop[:, par, j, c * CH + a:(c + 1) * CH], start=True, stop=not diagonal)
                        if diagonal:
                            mm = pe.matmul(pe_[:, bank, 0:P], keep["identr"][:, :], keep["mask_k"][:, :],
                                           start=False, stop=True)
                        mm.then_inc(e_scores, 1)
                        e += 1
                    if item[0] == "PV":
                        _, c, kb = item
                        a = P * max(0, kb - TB * c)
                        last = kb == TB * (c + 1) - 1
                        in_band = TB * c - kb <= BAND
                        pe.wait_ge(e_weights, E_UNITS * g + GH * (kq + 1) + EBANKS)
                        if kb == 0:
                            pe.wait_ge(o_kept, NC * g + c + 1)
                        if decayed:
                            for j in range(GH):
                                mm = pe.matmul(po[STRIP * j:STRIP * (j + 1), a:CH], keep["ones_strip"][:, :],
                                               wt[:, kq % buffers, j, a:CH], start=(kb == 0), stop=False)
                            if in_band:
                                band += GH
                                pe.wait_ge(w_decayed, BAND_UNITS * g + band)
                                a, z, _ = band_columns(c, kb)
                                for j in range(GH):
                                    mm = pe.matmul(po[STRIP * j:STRIP * (j + 1), a:z], va[:, par, kb, j, :],
                                                   wd[:, kq % 2, j, a:z], start=False, stop=last)
                        else:
                            if kb >= TB * c:
                                masked += 1
                                pe.wait_ge(w_masked, NC * TB * g + masked)
                            for j in range(GH):
                                mm = pe.matmul(po[STRIP * j:STRIP * (j + 1), a:CH], va[:, par, kb, j, :],
                                               wt[:, kq % buffers, j, a:CH], start=(kb == 0), stop=last)
                        mm.then_inc(pv_done, 1)
                        kq += 1

            steps(pe, step)


def band_columns(c, kb):
    a = P * max(0, kb - TB * c)
    z = min(CH, P * (kb - TB * c + BAND + 1))
    return a, z, P * (TB * c - kb) + a


def output_projection(nc, name, x_src, x_dst, xn_dst, w, norm, keep, dram):
    with ExitStack() as ctx:
        sb = lambda n, s, d: ctx.enter_context(nc.sbuf_tensor(f"{name}_{n}", s, d))
        sm = phase_semaphores(nc, ctx, name)
        wp = sb("wp", [P, NG, D], F32)
        gamma, beta = sb("gamma", [P, D], F32), sb("beta", [P, D], F32)
        y = sb("y", [P, 2, NG, CH], F32)
        yn = sb("yn", [P, 2, NG, CH], F32)
        sums = sb("sums", [P, 2, SUMS], F32)
        part = sb("part", [P, 2, SUMS], F32)
        spread = sb("spread", [P, 2, NG, CH], F32)
        x = sb("x", [P, 2, TB, D], F32)
        xb = sb("xb", [P, 2, TB, D], F32)
        zg = sb("zg", [P, 2, TB, D], F32)
        xo = sb("xo", [P, 2, TB, D], F32)
        xn = sb("xn", [P, 2, TB, D], F32)
        stats = sb("stats", [P, TB, 6], F32)
        mean, half = sb("mean", [P, 2, TB], F32), sb("half", [P, 2, TB], F32)
        var, sd, rs = (sb(n, [P, 2, TB], F32) for n in ("var", "sd", "rs"))
        pp = ctx.enter_context(nc.psum_tensor(f"{name}_pp", [P, 2, TB, D], F32))
        zeroed, w_in = sm("zeroed"), sm("w_in")
        y_in, x_in = ([sm(f"{n}{i}") for i in range(2)] for n in ("y_in", "x_in"))
        s_in, r_out, r_in = ([sm(f"{n}{i}") for i in range(2)] for n in ("s_in", "r_out", "r_in"))
        part_ready, yn_ready = sm("part_ready"), sm("yn_ready")
        projected, p_read, chain = sm("projected"), sm("p_read"), sm("chain")
        var_ready, sd_ready, xb_ready = sm("var_ready"), sm("sd_ready"), sm("xb_ready")
        xo_ready, xn_ready = sm("xo_ready"), sm("xn_ready")
        stored = [sm(f"stored{i}") for i in range(2)]
        block = ctx.enter_context(nc.Block())
        NW = 16 * (GH + 3 * bool(norm))
        NORMS = 2 if norm else 1

        @block.sync
        def _(sp):
            for par in range(2):
                sp.sem_inc(r_out[par], 16)

            def load_weights():
                sp.wait_ge(zeroed, 1)
                for j in range(GH):
                    sp.dma_start(wp[STRIP * j:STRIP * j + HD, :, :],
                                 w.rearrange("(g j d) n -> j d g n", j=GH, d=HD)[j]).then_inc(w_in, 16)
                if norm:
                    sp.dma_start(wp[HD:HD + 1, 0, :], row_of(norm[0])).then_inc(w_in, 16)
                    for t, src in zip((gamma, beta), norm[1:]):
                        sp.dma_start(t[:, :], row_of(src).to_broadcast([P, D])).then_inc(w_in, 16)

            def load_sums(b, c):
                G, par = NC * b + c, c % 2
                sp.wait_ge(part_ready, G + 1)
                for g in range(NG):
                    src = dram["y"][b + c // NC, g, c % NC].rearrange("(j r) (s t) -> r j s t", j=GH, t=SUMS)[HD]
                    dst = sums[g * STRIP:(g + 1) * STRIP, par, :]
                    sp.dma_start(dst, src).then_inc(s_in[par], 16)

            def load_y(b, c):
                G, par = NC * b + c, c % 2
                sp.wait_ge(yn_ready, G + 1)
                src = dram["y"][b + c // NC, :, c % NC].rearrange("g p t -> p g t")
                sp.dma_start(y[:, par, :, :], src).then_inc(y_in[par], 16)

            def load_spread(b, c):
                G, par = NC * b + c, c % 2
                part_d = at(dram["part"], b, c)
                sp.wait_ge(part_ready, G + 3)
                sp.dma_start(part_d, part[:, par, :]).then_inc(r_out[par], 16)
                sp.wait_ge(yn_ready, G + 1)
                sp.wait_ge(r_out[par], 16 * (2 * b + c // 2 + 2))
                for j in range(GH):
                    src = part_d.rearrange("(g j s) t -> j g (s t)", j=GH, g=NG)[j]
                    src = src.rearrange("(o g) q -> o g q", o=1).to_broadcast([STRIP, NG, CH])
                    sp.dma_start(spread[STRIP * j:STRIP * (j + 1), par, :, :], src).then_inc(r_in[par], 16)

            def load_x(b, c):
                G, par = NC * b + c, c % 2
                sp.wait_ge(xo_ready, G + 1)
                sp.dma_start(x[:, par, :, :], at(x_src, b, c)).then_inc(x_in[par], 16)

            def body(b, last):
                for c in range(NC):
                    if not last or c + 2 < NC:
                        load_y(b, c + 2)
                    if not last or c + 3 < NC:
                        load_sums(b, c + 3)
                    if not last or c + 2 < NC:
                        load_spread(b, c + 2)
                        load_x(b, c + 2)

            load_sums(0, 0)
            load_sums(0, 1)
            load_y(0, 0)
            load_weights()
            load_spread(0, 0)
            load_sums(0, 2)
            load_x(0, 0)
            load_y(0, 1)
            load_spread(0, 1)
            load_x(0, 1)
            sequences(sp, body)
        @block.gpsimd
        def _(pool):
            pool.memset(wp[:, :, :], 0.0).then_inc(zeroed, 1)
            if norm:
                pool.wait_ge(w_in, NW)
                with pool.Fori(0, B) as b:
                    for c in range(NC):
                        G, par = NC * b + c, c % 2
                        pool.wait_ge(x_in[par], 16 * (2 * b + c // 2 + 1))
                        pool.wait_ge(xo_ready, G + 1)
                        for t in range(TB):
                            s = pool.tensor_tensor(xb[:, par, t, :], x[:, par, t, :], beta[:, :], ALU.add)
                        s.then_inc(xb_ready, 1)

        @block.tensor
        def _(pe):
            pe.sem_inc(projected, 2)
            pe.wait_ge(w_in, NW)
            with pe.Fori(0, B) as b:
                for c in range(NC):
                    G, par = NC * b + c, c % 2
                    pe.wait_ge(yn_ready, G + 3)
                    pe.wait_ge(p_read if norm else xo_ready, G + 1)
                    for t in range(TB):
                        for g in range(NG):
                            mm = pe.matmul(pp[:, par, t, :], yn[:, par, g, t * P:(t + 1) * P], wp[:, g, :],
                                           start=(g == 0), stop=(g == NG - 1))
                    mm.then_inc(projected, 1)

        @block.scalar
        def _(act):
            for par in range(2):
                act.sem_inc(stored[par], 32)
            with act.Fori(0, B) as b:
                for c in range(NC):
                    G, par = NC * b + c, c % 2

                    def root(n):
                        act.wait_ge(var_ready, NORMS * G + n + 1)
                        act.activation(sd[:, par, :], var[:, par, :], ACT.Sqrt).then_inc(sd_ready, 1)

                    if norm:
                        root(0)
                    act.wait_ge(xo_ready, G + 3)
                    act.dma_start(x_dst[b, c], xo[:, par, :, :]).then_inc(stored[par], 16)
                    root(NORMS - 1)
                    act.wait_ge(xn_ready, G + 1)
                    act.dma_start(xn_dst[b, c], xn[:, par, :, :]).then_inc(stored[par], 16)
            for par in range(2):
                act.wait_ge(stored[par], 32 * (B * NC // 2 + 1))

        @block.vector
        def _(dve):
            dve.sem_inc(p_read, 2)
            dve.sem_inc(xo_ready, 2)

            def moments(G, par, src, n):
                first = 4 * (NORMS * G + n) + 1
                for t in range(TB):
                    s = dve.bn_stats(stats[:, t, :], src[:, par, t, :])
                s.then_inc(chain, 1)
                dve.wait_ge(chain, first)
                halves_sums(dve, stats, mean[:, par, :], half).then_inc(chain, 1)
                dve.wait_ge(chain, first + 1)
                halves_terms(dve, mean[:, par, :], half).then_inc(chain, 1)
                dve.wait_ge(chain, first + 2)
                halves_variance(dve, var[:, par, :], half).then_inc(var_ready, 1)
                dve.wait_ge(sd_ready, NORMS * G + n + 1)
                dve.reciprocal(rs[:, par, :], sd[:, par, :]).then_inc(chain, 1)
                dve.wait_ge(chain, first + 3)

            def invert(b, c):
                G, par = NC * b + c, c % 2
                dve.wait_ge(s_in[par], 16 * NG * (2 * b + c // 2 + 1))
                dve.wait_ge(r_out[par], 16 * (2 * b + c // 2 + 1))
                dve.reciprocal(part[:, par, :], sums[:, par, :]).then_inc(part_ready, 1)

            def divide(b, c):
                G, par = NC * b + c, c % 2
                dve.wait_ge(y_in[par], 16 * (2 * b + c // 2 + 1))
                dve.wait_ge(r_in[par], 16 * GH * (2 * b + c // 2 + 1))
                dve.wait_ge(projected, G + 1)
                dve.tensor_tensor(yn[:, par, :, :], y[:, par, :, :], spread[:, par, :, :], ALU.mult)\
                   .then_inc(yn_ready, 1)

            dve.sem_inc(part_ready, 2)
            dve.sem_inc(yn_ready, 2)

            def body(b, last):
                for c in range(NC):
                    G, par = NC * b + c, c % 2
                    if not last or c + 1 < NC:
                        divide(b, c + 1)
                    if not last or c + 2 < NC:
                        invert(b, c + 2)
                    dve.wait_ge(projected, G + 3)
                    if norm:
                        moments(G, par, pp, 0)
                        for t in range(TB):
                            s = dve.scalar_tensor_tensor(out=zg[:, par, t, :], in0=pp[:, par, t, :],
                                                         scalar=mean[:, par, t:t + 1], in1=gamma[:, :],
                                                         op0=ALU.subtract, op1=ALU.mult)
                        s.then_inc(p_read, 1)
                        dve.wait_ge(p_read, G + 3)
                        dve.wait_ge(xb_ready, G + 1)
                        dve.wait_ge(stored[par], 32 * (2 * b + c // 2 + 1))
                        for t in range(TB):
                            s = dve.scalar_tensor_tensor(out=xo[:, par, t, :], in0=zg[:, par, t, :],
                                                         scalar=rs[:, par, t:t + 1], in1=xb[:, par, t, :],
                                                         op0=ALU.mult, op1=ALU.add)
                        s.then_inc(xo_ready, 1)
                    else:
                        dve.wait_ge(x_in[par], 16 * (2 * b + c // 2 + 1))
                        dve.wait_ge(stored[par], 32 * (2 * b + c // 2 + 1))
                        for t in range(TB):
                            s = dve.tensor_tensor(xo[:, par, t, :], pp[:, par, t, :], x[:, par, t, :], ALU.add)
                        s.then_inc(xo_ready, 1)
                    dve.wait_ge(xo_ready, G + 3)
                    moments(G, par, xo, NORMS - 1)
                    for t in range(TB):
                        s = dve.tensor_scalar(xn[:, par, t, :], xo[:, par, t, :], mean[:, par, t:t + 1],
                                              rs[:, par, t:t + 1], ALU.subtract, ALU.mult)
                    s.then_inc(xn_ready, 1)

            invert(0, 0)
            invert(0, 1)
            divide(0, 0)
            dve.wait_ge(w_in, NW)
            sequences(dve, body)


def feed_forward(nc, name, x_src, xn_src, dst, keep):
    with ExitStack() as ctx:
        sb = lambda n, s, d: ctx.enter_context(nc.sbuf_tensor(f"{name}_{n}", s, d))
        ps = lambda n, s: ctx.enter_context(nc.psum_tensor(f"{name}_{n}", s, F32))
        sm = phase_semaphores(nc, ctx, name)
        GB = 4
        x = sb("x", [P, 2, TB, D], F32)
        xn = sb("xn", [P, 2, TB, D], F32)
        xt_hi, xt_lo = sb("xt_hi", [P, 2, KT, CH], F32R), sb("xt_lo", [P, 2, KT, CH], F32R)
        g = sb("g", [P, GB, CH], F32)
        g_hi, g_lo = sb("g_hi", [P, GB, CH], F32R), sb("g_lo", [P, GB, CH], F32R)
        o = sb("o", [P, KT, CH], F32)
        xo = sb("xo", [P, 2, TB, D], F32)
        pt, ph, po, pb = ps("pt", [P, KT, CH]), ps("ph", [P, 2, CH]), ps("po", [P, KT, CH]), ps("pb", [P, TB, D])
        xn_in, x_in = ([sm(f"{n}{i}") for i in range(2)] for n in ("xn_in", "x_in"))
        turned, hi_ready, lo_ready = sm("turned"), sm("hi_ready"), sm("lo_ready")
        h_done, g_ready, g_hi_ready, g_lo_ready = sm("h_done"), sm("g_ready"), sm("g_hi_ready"), sm("g_lo_ready")
        g_used, o_kept, back, xo_ready = sm("g_used"), sm("o_kept"), sm("back"), sm("xo_ready")
        stored = [sm(f"stored{i}") for i in range(2)]
        block = ctx.enter_context(nc.Block())

        @block.sync
        def _(sp):
            for par in range(2):
                sp.sem_inc(stored[par], 16)

            def store(b, c):
                sp.wait_ge(xo_ready, NC * b + c + 3)
                sp.dma_start(dst[b, c], xo[:, c % 2, :, :]).then_inc(stored[c % 2], 16)

            def load(b, c):
                G, par = NC * b + c, c % 2
                sp.wait_ge(turned, G + 1)
                sp.dma_start(xn[:, par, :, :], at(xn_src, b, c)).then_inc(xn_in[par], 16)
                sp.wait_ge(xo_ready, G + 1)
                sp.dma_start(x[:, par, :, :], at(x_src, b, c)).then_inc(x_in[par], 16)

            def body(b, last):
                for c in range(NC):
                    store(b, c)
                    if not last or c + 2 < NC:
                        load(b, c + 2)

            load(0, 0)
            load(0, 1)
            sequences(sp, body)
            for par in range(2):
                sp.wait_ge(stored[par], 16 * (B * NC // 2 + 1))

        @block.tensor
        def _(pe):
            pe.sem_inc(turned, 2)
            pe.sem_inc(g_used, GB)
            pe.sem_inc(back, 1)

            def turn(b, c):
                G, par = NC * b + c, c % 2
                pe.wait_ge(xn_in[par], 16 * (2 * b + c // 2 + 1))
                pe.wait_ge(lo_ready, G + 1)
                for t in range(TB):
                    for kt in range(KT):
                        mm = pe.transpose(pt[:, kt, t * P:(t + 1) * P], xn[:, par, t, kt * P:(kt + 1) * P],
                                          keep["ident"][:, :])
                mm.then_inc(turned, 1)

            def hidden(b, c, h):
                G, par = NC * b + c, c % 2
                pe.wait_ge(g_ready, HT * G + h + 1)
                n = 0
                for kt in range(KT):
                    for part in (xt_hi, xt_lo):
                        mm = pe.matmul(ph[:, h % 2, :], keep["w1s"][:, kt, h * P:(h + 1) * P], part[:, par, kt, :],
                                       start=(n == 0), stop=(n == 2 * KT - 1))
                        n += 1
                mm.then_inc(h_done, 1)

            def output(b, c, h):
                G = NC * b + c
                pe.wait_ge(g_lo_ready, HT * G + h + GB + 1)
                if h == 0:
                    pe.wait_ge(o_kept, G + 1)
                for part, ready in ((g_hi, g_hi_ready), (g_lo, g_lo_ready)):
                    for kt in range(KT):
                        mm = pe.matmul(po[:, kt, :], keep["w2s"][:, h, kt * P:(kt + 1) * P],
                                       part[:, h % GB, :],
                                       start=(h == 0 and part is g_hi), stop=(h == HT - 1 and part is g_lo))
                mm.then_inc(g_used, 1)

            def turn_back(b, c):
                G = NC * b + c
                pe.wait_ge(o_kept, G + 2)
                pe.wait_ge(xo_ready, G + 2)
                for t in range(TB):
                    for kt in range(KT):
                        mm = pe.transpose(pb[:, t, kt * P:(kt + 1) * P], o[:, kt, t * P:(t + 1) * P],
                                          keep["ident"][:, :])
                mm.then_inc(back, 1)

            def begin(b, c):
                G = NC * b + c
                pe.wait_ge(hi_ready, G + 1)
                pe.wait_ge(lo_ready, G + 2)

            def body(b, last):
                for c in range(NC):
                    follows = not last or c + 1 < NC
                    for h in range(HT):
                        if 1 <= h < HT - 2:
                            hidden(b, c, h + 2)
                        elif h >= HT - 2 and follows:
                            if h == HT - 2:
                                begin(b, c + 1)
                            hidden(b, c + 1, h + 2 - HT)
                        output(b, c, h)
                        if h == 2 and follows:
                            turn(b, c + 1)
                    if follows:
                        hidden(b, c + 1, 2)
                    turn_back(b, c)

            turn(0, 0)
            begin(0, 0)
            for h in range(EARLY):
                hidden(0, 0, h)
            sequences(pe, body)

        @block.scalar
        def _(act):
            act.sem_inc(g_ready, 2)
            act.sem_inc(o_kept, 1)

            def parts(b, c):
                G, par = NC * b + c, c % 2
                act.wait_ge(turned, G + 3)
                act.activation(xt_hi[:, par, :, :], pt[:, :, :], ACT.Copy).then_inc(hi_ready, 1)

            def leave(b, c):
                G = NC * b + c
                act.wait_ge(g_used, HT * G + HT + GB)
                act.wait_ge(back, G + 1)
                for kt in range(KT):
                    s = act.activation(o[:, kt, :], po[:, kt, :], ACT.Identity, bias=keep["b2"][:, kt:kt + 1],
                                       scale=keep["alpha2"][:, kt:kt + 1])
                s.then_inc(o_kept, 1)

            def hidden(b, c, h):
                G = NC * b + c
                act.wait_ge(h_done, HT * G + h + 1)
                act.wait_ge(g_lo_ready, HT * G + h + 1)
                act.activation(g[:, h % GB, :], ph[:, h % 2, :], ACT.Gelu, bias=keep["b1"][:, h:h + 1],
                               scale=keep["alpha1"][:, h:h + 1]).then_inc(g_ready, 1)

            def body(b, last):
                for c in range(NC):
                    follows = not last or c + 1 < NC
                    for h in range(EARLY, HT):
                        hidden(b, c, h)
                        if h == 5 and follows:
                            parts(b, c + 1)
                    for h in range(EARLY):
                        if h == EARLY - 1:
                            leave(b, c)
                        if follows:
                            hidden(b, c + 1, h)

            parts(0, 0)
            for h in range(EARLY):
                hidden(0, 0, h)
            sequences(act, body)

        @block.vector
        def _(dve):
            dve.sem_inc(lo_ready, 1)
            dve.sem_inc(g_lo_ready, GB)
            dve.sem_inc(xo_ready, 2)

            def add(b, c):
                G, par = NC * b + c, c % 2
                dve.wait_ge(back, G + 2)
                dve.wait_ge(x_in[par], 16 * (2 * b + c // 2 + 1))
                dve.wait_ge(stored[par], 16 * (2 * b + c // 2 + 1))
                dve.tensor_tensor(xo[:, par, :, :], pb[:, :, :], x[:, par, :, :], ALU.add).then_inc(xo_ready, 1)

            def parts(b, c):
                G, par = NC * b + c, c % 2
                dve.wait_ge(hi_ready, G + 1)
                dve.tensor_tensor(xt_lo[:, par, :, :], pt[:, :, :], xt_hi[:, par, :, :].bitcast(F32),
                                  ALU.subtract).then_inc(lo_ready, 1)

            def split(b, c, h):
                G = NC * b + c
                dve.wait_ge(g_ready, HT * G + h + 3)
                dve.wait_ge(g_used, HT * G + h + 1)
                dve.tensor_copy(g_hi[:, h % GB, :], g[:, h % GB, :]).then_inc(g_hi_ready, 1)
                dve.wait_ge(g_hi_ready, HT * G + h + 1)
                dve.tensor_tensor(g_lo[:, h % GB, :], g[:, h % GB, :], g_hi[:, h % GB, :].bitcast(F32),
                                  ALU.subtract).then_inc(g_lo_ready, 1)

            def body(b, last):
                for c in range(NC):
                    follows = not last or c + 1 < NC
                    for h in range(EARLY, HT):
                        split(b, c, h)
                        if h == 5 and follows:
                            parts(b, c + 1)
                    if follows:
                        for h in range(EARLY):
                            split(b, c + 1, h)
                    add(b, c)

            parts(0, 0)
            for h in range(EARLY):
                split(0, 0, h)
            sequences(dve, body)


INPUTS = ["L0_attn_a_x", "L0_attn_a_W_attn", "L0_attn_a_W_proj", "L0_attn_b_Wq", "L0_attn_b_bq", "L0_attn_b_Wk",
          "L0_attn_b_bk", "L0_attn_b_Wv", "L0_attn_b_bv", "L0_attn_b_Wo", "L0_attn_b_bo", "L0_attn_b_gamma",
          "L0_attn_b_beta", "L0_ffn_w1", "L0_ffn_b1", "L0_ffn_w2", "L0_ffn_b2"]


def build(nc, t, decay, out):
    def chunks(a):
        return a.rearrange("b (c t p) d -> b c p t d", t=TB, p=P)

    with ExitStack() as ctx:
        def dram(n, shape, dt):
            return nc.dram_tensor(n, shape, dt, kind="Internal").ap()

        def sb(n, shape, dt):
            return ctx.enter_context(nc.sbuf_tensor(n, shape, dt))

        x = [chunks(t["L0_attn_a_x"])] + [chunks(dram(f"x{i}", (B, T, D), F32)) for i in range(1, 4)] + [chunks(out)]
        xn = chunks(dram("xn", (B, T, D), F32))
        scratch = {
            "qk": dram("qk", (B, NG, 2, 2, GH * HD, T), F32),
            "v": dram("v", (B, NG, NC, P, TB * GH * STRIP), F32),
            "y": dram("y", (B, NG, NC, P, CH), F32),
            "part": dram("part", (B, NC, P, SUMS), F32),
        }
        keep = {
            "ident": sb("ident", [P, P], F32), "identr": sb("identr", [P, P], F32R),
            "mask_q": sb("mask_q", [P, P], F32R), "mask_k": sb("mask_k", [P, P], F32R),
            "ones_strip": sb("ones_strip", [P, STRIP], F32),
            "decay": sb("decay", [P, DECAY_COLS], F32),
            "w1s": sb("w1s", [P, KT, FF], F32R), "w2s": sb("w2s", [P, HT, D], F32R),
            "alpha1": sb("alpha1", [P, HT], F32), "alpha2": sb("alpha2", [P, KT], F32),
            "b1": sb("b1", [P, HT], F32), "b2": sb("b2", [P, KT], F32),
        }
        ffn = {"w1": t["L0_ffn_w1"], "b1": t["L0_ffn_b1"], "w2": t["L0_ffn_w2"], "b2": t["L0_ffn_b2"], "decay": decay}
        setup(nc, ffn, keep)
        projections(nc, "qkv_a", x[0], [(t["L0_attn_a_W_attn"], (0, 3 * D))], None, False, keep, scratch)
        attention(nc, "att_a", True, keep, scratch)
        output_projection(nc, "out_a", x[0], x[1], xn, t["L0_attn_a_W_proj"], None, keep, scratch)
        feed_forward(nc, "ffn_a", x[1], xn, x[2], keep)
        projections(nc, "qkv_b", x[2], [(t[f"L0_attn_b_W{n}"], (i * D, (i + 1) * D)) for i, n in enumerate("qkv")],
                    [t[f"L0_attn_b_b{n}"] for n in "qkv"], True, keep, scratch)
        attention(nc, "att_b", False, keep, scratch)
        output_projection(nc, "out_b", x[2], x[3], xn, t["L0_attn_b_Wo"],
                          [t[f"L0_attn_b_{n}"] for n in ("bo", "gamma", "beta")], keep, scratch)
        feed_forward(nc, "ffn_b", x[3], xn, x[4], keep)


def kernel(**inputs):
    import concourse.bacc as bacc
    from concourse.bass_utils import run_bass_kernel_spmd

    nc = bacc.Bacc("TRN2", target_bir_lowering=False, num_devices=1)
    arrays = {f"in_{n}": np.ascontiguousarray(inputs[n]) for n in INPUTS}
    t = {n: nc.dram_tensor(f"in_{n}", arrays[f"in_{n}"].shape, F32, kind="ExternalInput").ap() for n in INPUTS}
    arrays["decay_table"] = decay_table()
    decay = nc.dram_tensor("decay_table", arrays["decay_table"].shape, F32, kind="ExternalInput").ap()
    out = nc.dram_tensor("out", (B, T, D), F32, kind="ExternalOutput").ap()
    nc.disable_value_cache = True
    build(nc, t, decay, out)
    return run_bass_kernel_spmd(nc, [arrays], core_ids=[0]).results[0]["out"]
```

```python
from contextlib import ExitStack

import numpy as np
import concourse.bass as bass
from concourse import mybir

ALU = mybir.AluOpType
ACT = mybir.ActivationFunctionType
AX = mybir.AxisListType
F32 = mybir.dt.float32
F32R = mybir.dt.float32r
BF16 = mybir.dt.bfloat16

P = 128
B, T, D = 2, 2048, 256
H, HD = 16, 16
FF = 1024
KT = D // P
HT = FF // P
CH = 512
NC = T // CH
TB = CH // P
GH = 4
NG = H // GH
GROUPS = B * NG
STRIP = P // GH
SUMS = H * CH // P
BLOCKS = T // P
SCALE = HD ** -0.5
EPS = 1e-5
MASK = -1e37
PAIRS = 4
MROW = PAIRS * HD
ECHOIC, DECAY_LENGTH = 16, 512
SPAN = DECAY_LENGTH - 1
BAND = SPAN // P + 1
DECAY_COLS = (BAND + 1) * P
PV_TIME = 400.0
LEAD, LEAD_DECAYED = 0.45, 0.38
EARLY = 3


def decay_table():
    dl = DECAY_LENGTH - ECHOIC + 1
    nums = np.linspace(0.0, 1.0, dl, dtype=np.float32)
    values = (1.0 - np.power(nums, np.float32(1.0 / np.e))).astype(np.float32)
    values = np.concatenate([np.ones(ECHOIC - 1, np.float32), values])
    lag = np.arange(DECAY_COLS)[None, :] - np.arange(P)[:, None]
    return np.where(lag < 0, 0, values[np.clip(lag, 0, DECAY_LENGTH - 1)]).astype(np.float32)


def row_of(vector):
    return vector.rearrange("(a n) -> a n", a=1)


def columns_of(vector):
    return vector.rearrange("(t p) -> p t", p=P)


def phase_semaphores(nc, ctx, name):
    taken = []

    def give_back():
        nc.clear_and_free_semaphores(taken)
        nc.all_engine_barrier()

    def take(n):
        taken.append(nc.alloc_semaphore(name=f"{name}_{n}"))
        return taken[-1]

    ctx.callback(give_back)
    return take


def sequences(eng, body):
    with eng.Fori(0, B - 1) as b:
        body(b, False)
    body(B - 1, True)


def at(chunks, b, c):
    return chunks[b + c // NC, c % NC]


def setup(nc, io, keep, dram):
    with ExitStack() as ctx:
        sb = lambda n, s, d: ctx.enter_context(nc.sbuf_tensor(n, s, d))
        w1 = sb("w1_rows", [P, HT, D], F32)
        w2 = sb("w2_rows", [P, KT, FF], F32)
        neg = sb("w_negative", [P, HT, D], F32)
        sign1 = sb("w1_sign", [P, HT, D], F32)
        sign2 = sb("w2_sign", [P, KT, FF], F32)
        w1s, w2s = sb("w1_signs", [P, KT, FF], F32R), sb("w2_signs", [P, HT, D], F32R)
        turned = ctx.enter_context(nc.psum_tensor("w_turned", [P, 4, CH], F32))
        sem = phase_semaphores(nc, ctx, "setup")
        w_loaded, ident_ready, zeroed = sem("w_loaded"), sem("ident_ready"), sem("zeroed")
        sign_step, signs_ready = sem("sign_step"), sem("signs_ready")
        w_turned, w_kept = sem("w_turned_sem"), sem("w_kept")
        const_loaded, signs_out = sem("const_loaded"), sem("signs_out")
        ident, identr = keep["ident"], keep["identr"]
        block = ctx.enter_context(nc.Block())

        @block.sync
        def _(sp):
            sp.dma_start(w1[:, :, :], io["w1"].rearrange("(t p) d -> p t d", p=P)).then_inc(w_loaded, 16)
            sp.dma_start(w2[:, :, :], io["w2"].rearrange("(t p) d -> p t d", p=P)).then_inc(w_loaded, 16)
            with nc.allow_non_contiguous_dma(reason="biases as columns, once"):
                sp.dma_start(keep["b1"][:, :], columns_of(io["b1"])).then_inc(const_loaded, 16)
                sp.dma_start(keep["b2"][:, :], columns_of(io["b2"])).then_inc(const_loaded, 16)
            sp.dma_start(keep["decay"][:, :], io["decay"]).then_inc(const_loaded, 16)
            sp.wait_ge(const_loaded, 48)
            sp.wait_ge(w_kept, 4)
            sp.dma_start(dram["w1s"], w1s[:, :, :].bitcast(F32)).then_inc(signs_out, 16)
            sp.wait_ge(w_kept, 8)
            sp.dma_start(dram["w2s"], w2s[:, :, :].bitcast(F32)).then_inc(signs_out, 16)
            sp.wait_ge(signs_out, 32)

        @block.gpsimd
        def _(pool):
            pool.memset(ident[:, :], 0.0).then_inc(zeroed, 1)
            pool.memset(identr[:, :].bitcast(F32), 0.0).then_inc(zeroed, 1)
            pool.memset(keep["mask_q"][:, :].bitcast(F32), 0.0).then_inc(zeroed, 1)
            pool.memset(keep["mask_k"][:, :].bitcast(F32), 0.0).then_inc(zeroed, 1)
            pool.memset(keep["ones_strip"][:, 0:HD], 0.0).then_inc(zeroed, 1)
            pool.memset(keep["ones_strip"][:, HD:STRIP], 1.0).then_inc(zeroed, 1)
            pool.wait_ge(zeroed, 6)
            for m in (ident, identr):
                pool.affine_select(out=m[:, :], in_=m[:, :].bitcast(F32), compare_op=ALU.not_equal, fill=1.0, base=0,
                                   pattern=[[-1, P]], channel_multiplier=1).then_inc(ident_ready, 1)
            pool.affine_select(out=keep["mask_q"][:, :], in_=keep["mask_q"][:, :].bitcast(F32), compare_op=ALU.is_ge,
                               fill=MASK, base=0, pattern=[[-1, P]], channel_multiplier=1).then_inc(ident_ready, 1)
            pool.affine_select(out=keep["mask_k"][:, :], in_=keep["mask_k"][:, :].bitcast(F32), compare_op=ALU.is_ge,
                               fill=MASK, base=0, pattern=[[1, P]], channel_multiplier=-1).then_inc(ident_ready, 1)

        @block.vector
        def _(dve):
            dve.wait_ge(w_loaded, 32)
            for w, s, n, tiles, alpha in ((w1, sign1, D, HT, keep["alpha1"]), (w2, sign2, FF, KT, keep["alpha2"])):
                step = 4 * (w is w2)
                below = neg[:, :, :].rearrange("p a b -> p (a b)").rearrange("p (t d) -> p t d", t=tiles)
                dve.tensor_reduce(alpha[:, :], w[:, :, :], AX.X, ALU.add,
                                  apply_absolute_value=True).then_inc(sign_step, 1)
                dve.wait_ge(sign_step, step + 1)
                dve.tensor_scalar(alpha[:, :], alpha[:, :], 1.0 / n, None, ALU.mult).then_inc(sign_step, 1)
                dve.wait_ge(sign_step, step + 2)
                dve.tensor_scalar(below, w[:, :, :], 0.0, None, ALU.is_lt).then_inc(sign_step, 1)
                dve.wait_ge(sign_step, step + 3)
                dve.scalar_tensor_tensor(out=s[:, :, :], in0=w[:, :, :], scalar=0.0, in1=below,
                                         op0=ALU.is_gt, op1=ALU.subtract).then_inc(sign_step, 1)
                dve.wait_ge(sign_step, step + 4)
            dve.sem_inc(signs_ready, 1)
            for n in range(8):
                dve.wait_ge(w_turned, n + 1)
                if n < 4:
                    kt, half = n // 2, n % 2
                    dst = w1s[:, kt, half * CH:(half + 1) * CH]
                    dve.tensor_copy(dst, turned[:, n % 4, :]).then_inc(w_kept, 1)
                else:
                    ht = 2 * (n - 4)
                    dst = w2s[:, ht:ht + 2, :]
                    dve.tensor_copy(dst, turned[:, n % 4, :].rearrange("p (a d) -> p a d", a=2)).then_inc(w_kept, 1)

        @block.tensor
        def _(pe):
            pe.wait_ge(ident_ready, 1)
            pe.wait_ge(signs_ready, 1)
            for n in range(8):
                if n >= 4:
                    pe.wait_ge(w_kept, n - 3)
                for q in range(4):
                    if n < 4:
                        kt, half = n // 2, n % 2
                        src = sign1[:, 4 * half + q, kt * P:(kt + 1) * P]
                    else:
                        ht = 2 * (n - 4) + q // 2
                        src = sign2[:, q % 2, ht * P:(ht + 1) * P]
                    mm = pe.transpose(turned[:, n % 4, q * P:(q + 1) * P], src, ident[:, :])
                mm.then_inc(w_turned, 1)


def halves_sums(dve, stats, mean, half):
    dve.tensor_tensor(mean, stats[:, :, 1], stats[:, :, 4], ALU.add)
    dve.tensor_tensor(half[:, 0, :], stats[:, :, 1], stats[:, :, 4], ALU.subtract)
    return dve.tensor_tensor(half[:, 1, :], stats[:, :, 2], stats[:, :, 5], ALU.add)


def halves_terms(dve, mean, half):
    dve.tensor_scalar(mean, mean, 0.5, None, ALU.mult)
    dve.tensor_tensor(half[:, 0, :], half[:, 0, :], half[:, 0, :], ALU.mult)
    return dve.tensor_scalar(half[:, 1, :], half[:, 1, :], 1.0 / D, EPS, ALU.mult, ALU.add)


def halves_variance(dve, var, half):
    return dve.scalar_tensor_tensor(out=var, in0=half[:, 0, :], scalar=0.25, in1=half[:, 1, :],
                                    op0=ALU.mult, op1=ALU.add)


def projections(nc, name, x_dram, weights, biases, v_ones, keep, dram):
    with ExitStack() as ctx:
        sb = lambda n, s, d: ctx.enter_context(nc.sbuf_tensor(f"{name}_{n}", s, d))
        ps = lambda n, s: ctx.enter_context(nc.psum_tensor(f"{name}_{n}", s, F32))
        sm = phase_semaphores(nc, ctx, name)
        wqkv = sb("wqkv", [P, KT, 3 * D], F32)
        bqk = sb("bqk", [P, 2 * KT], F32)
        bv = sb("bv", [P, D], F32)
        x = sb("x", [P, 2, TB, D], F32)
        xn = sb("xn", [P, 2, TB, D], F32)
        xt = sb("xt", [P, 2, KT, CH], F32)
        stats = sb("stats", [P, 2, TB, 6], F32)
        mean, half = sb("mean", [P, 2, TB], F32), sb("half", [P, 2, TB], F32)
        var = sb("var", [P, 2, TB], F32)
        sd = sb("sd", [P, 2, TB], F32)
        rs = sb("rs", [P, 2, TB], F32)
        qk_hi = sb("qk_hi", [P, 2, 2 * KT, CH], F32R)
        qk_lo = sb("qk_lo", [P, 2, 2 * KT, CH], F32R)
        vt = sb("vt", [P, 2, TB, H, STRIP], F32)
        pt = ps("pt", [P, KT, CH])
        pqk = ps("pqk", [P, 2 * KT, CH])
        pv = ps("pv", [P, TB, D])
        w_scaled = sm("w_scaled")
        w_in, x_in, chain = sm("w_in"), [sm("x_in0"), sm("x_in1")], sm("chain")
        var_ready, sd_ready, xn_ready = sm("var_ready"), sm("sd_ready"), sm("xn_ready")
        turned, xt_ready, qk_done, v_done = sm("turned"), sm("xt_ready"), sm("qk_done"), sm("v_done")
        hi_ready, lo_ready, v_kept, vt_filled = sm("hi_ready"), sm("lo_ready"), sm("v_kept"), sm("vt_filled")
        stored = [sm(f"stored{i}") for i in range(2)]
        block = ctx.enter_context(nc.Block())
        M = 2 * KT
        STORE = 16 * (8 + NG)
        N_W = 16 * (len(weights) + 3 * bool(biases))

        @block.sync
        def _(sp):
            def load(b, c):
                sp.wait_ge(xn_ready, NC * b + c + 1)
                sp.dma_start(x[:, c % 2, :, :], at(x_dram, b, c)).then_inc(x_in[c % 2], 16)

            load(0, 0)
            for src, (a, z) in weights:
                sp.dma_start(wqkv[:, :, a:z], src.rearrange("(t p) n -> p t n", p=P)).then_inc(w_in, 16)
            if biases:
                with nc.allow_non_contiguous_dma(reason="biases as columns, once"):
                    sp.dma_start(bqk[:, 0:KT], columns_of(biases[0])).then_inc(w_in, 16)
                    sp.dma_start(bqk[:, KT:M], columns_of(biases[1])).then_inc(w_in, 16)
                sp.dma_start(bv[:, :], row_of(biases[2]).to_broadcast([P, D])).then_inc(w_in, 16)
            for par in range(2):
                sp.sem_inc(stored[par], STORE)

            def store(b, c):
                G, par = NC * b + c, c % 2
                sp.wait_ge(hi_ready, M * G + M)
                sp.wait_ge(lo_ready, M * G + 2 * M)
                for hl, t in ((0, qk_hi), (1, qk_lo)):
                    for a in range(2):
                        for qk in range(2):
                            dst = dram["qk"][b, :, hl, qk, :, c * CH:(c + 1) * CH]
                            dst = dst.rearrange("(m a) p t -> a p m t", a=2)[a]
                            sp.dma_start(dst, t[64 * a:64 * a + 64, par, KT * qk:KT * qk + KT, :].bitcast(F32))\
                              .then_inc(stored[par], 16)
                sp.wait_ge(v_kept, G + 2)
                for gh in range(NG):
                    sp.dma_start(dram["v"][b, gh, c].rearrange("p (t j e) -> p t j e", t=TB, j=GH),
                                 vt[:, par, :, GH * gh:GH * gh + GH, :]).then_inc(stored[par], 16)

            load(0, 1)

            def body(b, last):
                for c in range(NC):
                    if not last or c + 2 < NC:
                        load(b, c + 2)
                    store(b, c)

            sequences(sp, body)
            for par in range(2):
                sp.wait_ge(stored[par], STORE * (B * NC // 2 + 1))

        @block.gpsimd
        def _(pool):
            for par in range(2):
                pool.memset(vt[:, par, :, :, HD:STRIP], 1.0 if v_ones else 0.0).then_inc(vt_filled, 1)

        @block.vector
        def _(dve):
            dve.sem_inc(xn_ready, 2)
            dve.sem_inc(lo_ready, M)
            dve.sem_inc(v_kept, 1)

            def normalise(b, c):
                G, par = NC * b + c, c % 2
                dve.wait_ge(x_in[par], 16 * (2 * b + c // 2 + 1))
                for t in range(TB):
                    s = dve.bn_stats(stats[:, par, t, :], x[:, par, t, :])
                s.then_inc(chain, 1)
                dve.wait_ge(chain, 4 * G + 1)
                halves_sums(dve, stats[:, par, :, :], mean[:, par, :], half).then_inc(chain, 1)
                dve.wait_ge(chain, 4 * G + 2)
                halves_terms(dve, mean[:, par, :], half).then_inc(chain, 1)
                dve.wait_ge(chain, 4 * G + 3)
                halves_variance(dve, var[:, par, :], half).then_inc(var_ready, 1)
                dve.wait_ge(sd_ready, G + 1)
                dve.reciprocal(rs[:, par, :], sd[:, par, :]).then_inc(chain, 1)
                dve.wait_ge(chain, 4 * G + 4)
                dve.wait_ge(turned, G + 1)
                for t in range(TB):
                    s = dve.tensor_scalar(xn[:, par, t, :], x[:, par, t, :], mean[:, par, t:t + 1],
                                          rs[:, par, t:t + 1], ALU.subtract, ALU.mult)
                s.then_inc(xn_ready, 1)

            def finish(b, c):
                G, par = NC * b + c, c % 2
                dve.wait_ge(stored[par], STORE * (2 * b + c // 2 + 1))
                for m in range(M):
                    dve.wait_ge(hi_ready, M * G + m + 1)
                    dve.scalar_tensor_tensor(out=qk_lo[:, par, m, :], in0=pqk[:, m, :],
                                             scalar=bqk[:, m:m + 1] if biases else 0.0,
                                             in1=qk_hi[:, par, m, :].bitcast(F32), op0=ALU.add,
                                             op1=ALU.subtract).then_inc(lo_ready, 1)
                dve.wait_ge(v_done, G + 3)
                for t in range(TB):
                    src = pv[:, t, :].rearrange("p (h e) -> p h e", e=HD)
                    if biases:
                        s = dve.tensor_tensor(vt[:, par, t, :, 0:HD], src,
                                              bv[:, :].rearrange("p (h e) -> p h e", e=HD), ALU.add)
                    else:
                        s = dve.tensor_copy(vt[:, par, t, :, 0:HD], src)
                s.then_inc(v_kept, 1)

            def body(b, last):
                for c in range(NC):
                    if not last or c + 1 < NC:
                        normalise(b, c + 1)
                    finish(b, c)

            normalise(0, 0)
            dve.wait_ge(w_in, N_W)
            s = dve.tensor_scalar(wqkv[:, :, 0:D], wqkv[:, :, 0:D], SCALE, None, ALU.mult)
            if biases:
                s = dve.tensor_scalar(bqk[:, 0:KT], bqk[:, 0:KT], SCALE, None, ALU.mult)
            s.then_inc(w_scaled, 1)
            dve.wait_ge(w_scaled, 1)
            dve.wait_ge(vt_filled, 2)
            sequences(dve, body)

        @block.scalar
        def _(act):
            act.sem_inc(xt_ready, 1)

            def root(b, c):
                G, par = NC * b + c, c % 2
                act.wait_ge(var_ready, G + 1)
                act.activation(sd[:, par, :], var[:, par, :], ACT.Sqrt).then_inc(sd_ready, 1)

            def body(b, last):
                for c in range(NC):
                    G, par = NC * b + c, c % 2
                    act.wait_ge(turned, G + 3)
                    act.wait_ge(v_done, G + 1)
                    act.activation(xt[:, par, :, :], pt[:, :, :], ACT.Copy).then_inc(xt_ready, 1)
                    if not last or c + 1 < NC:
                        root(b, c + 1)
                    act.wait_ge(stored[par], STORE * (2 * b + c // 2 + 1))
                    for m in range(M):
                        act.wait_ge(qk_done, M * G + m + 1)
                        if biases:
                            act.activation(qk_hi[:, par, m, :], pqk[:, m, :], ACT.Identity,
                                           bias=bqk[:, m:m + 1]).then_inc(hi_ready, 1)
                        else:
                            act.activation(qk_hi[:, par, m, :], pqk[:, m, :], ACT.Copy).then_inc(hi_ready, 1)

            root(0, 0)
            act.wait_ge(w_scaled, 1)
            sequences(act, body)

        @block.tensor
        def _(pe):
            pe.sem_inc(turned, 2)
            pe.sem_inc(v_done, 2)

            def turn(b, c):
                G, par = NC * b + c, c % 2
                pe.wait_ge(xn_ready, G + 3)
                pe.wait_ge(xt_ready, G + 1)
                for t in range(TB):
                    for kt in range(KT):
                        mm = pe.transpose(pt[:, kt, t * P:(t + 1) * P], xn[:, par, t, kt * P:(kt + 1) * P],
                                          keep["ident"][:, :])
                mm.then_inc(turned, 1)

            def body(b, last):
                for c in range(NC):
                    G, par = NC * b + c, c % 2
                    pe.wait_ge(xt_ready, G + 2)
                    for m in range(M):
                        pe.wait_ge(lo_ready, M * G + m + 1)
                        for kt in range(KT):
                            mm = pe.matmul(pqk[:, m, :], wqkv[:, kt, m * P:(m + 1) * P], xt[:, par, kt, :],
                                           start=(kt == 0), stop=(kt == KT - 1))
                        mm.then_inc(qk_done, 1)
                        if m == 2 and (not last or c + 1 < NC):
                            turn(b, c + 1)
                    pe.wait_ge(v_kept, G + 1)
                    for t in range(TB):
                        for kt in range(KT):
                            mm = pe.matmul(pv[:, t, :], xt[:, par, kt, t * P:(t + 1) * P],
                                           wqkv[:, kt, 2 * D:3 * D], start=(kt == 0), stop=(kt == KT - 1))
                    mm.then_inc(v_done, 1)

            turn(0, 0)
            pe.wait_ge(w_in, N_W)
            pe.wait_ge(w_scaled, 1)
            sequences(pe, body)


UNITS = GH * TB
M_UNITS = UNITS * sum(c + 1 for c in range(NC))
FAR_UNITS = UNITS * sum(max(0, c - 1) for c in range(NC))


def near(c, decayed):
    return range(TB * max(0, c - 1) if decayed else 0, TB * (c + 1))


def far(c, decayed):
    return range(max(0, c - 1) if decayed else 0)


def attention_plan(weights, rest, ahead, decayed):
    e, m = [], []
    order = [(c, kb) for c in range(NC) for kb in near(c, decayed)]
    due = {}

    def follow(number, j, item):
        cost = PV_TIME if item[0] != "O" else 0.0
        due.setdefault((number, j) if number < len(order) else None, []).append((cost, item))

    for number, (c, kb) in enumerate(order):
        if decayed:
            follow(number + 1, GH - 1, ("PO", c, kb))
            follow(number + 2, GH // 2 - 1, ("PV", c, kb))
        else:
            follow(number + 1, GH - 1, ("PV", c, kb))
        if kb == near(c, decayed)[-1]:
            follow(number + 2, GH // 2 if decayed else GH // 2 - 1, ("O", c))
    for number, (c, kb) in enumerate(order):
        for j in range(GH):
            e.append((60.0 + CH - P * max(0, kb - TB * c), ("S", c, kb, j)))
            e += due.get((number, j), [])
    e += due[None]
    n = 0
    for c in range(NC):
        units = []
        for qb in range(TB):
            for j in range(GH):
                for piece in range(c + 1):
                    units.append((60.0 + (CH if piece < c else P * (qb + 1)), ("M", n, c, qb, j, piece)))
                    n += 1
        m += units + [(0.0, ("MF", c))]
    m = spaced(m, decayed)
    total_e, total_m = sum(x for x, _ in e), sum(x for x, _ in m)
    timed, at = [], 0.0
    for cost, item in e if weights else ():
        at += cost
        timed.append((at / total_e, 0, len(timed), item))
    at = 0.0
    for cost, item in m:
        at += cost
        t = at / total_m - (LEAD_DECAYED if decayed else LEAD)
        if t < 0 and ahead:
            timed.append((1 + t, 2, len(timed), (item[0], 1, *item[1:])))
        if t >= 0 and rest:
            timed.append((t, 1, len(timed), (item[0], 0, *item[1:])))
    return [item for _, _, _, item in sorted(timed)]


def spaced(m, decayed):
    out, late = [], []

    def follow(*items):
        late.extend([delay, cost, item] for delay, cost, item in items)

    for cost, item in m:
        out.append((cost, item))
        for x in late:
            x[0] -= 1
        out += [(x[1], x[2]) for x in late if x[0] == 0]
        late[:] = [x for x in late if x[0] > 0]
        if item[0] == "M" and item[5] in far(item[2], decayed):
            follow((1, 0.0, ("FX", *item[1:])))
        if item[0] == "MF":
            c = item[1]
            follow((3, 400.0, ("MT", c)), (6, 400.0, ("MC", c)))
            if far(c, decayed):
                follow((8, 0.0, ("FE", c)), (11, 0.0, ("FM", c)), (14, 200.0, ("FT", c)), (17, 200.0, ("FC", c)))
    return out + [(200.0, x[2]) for x in sorted(late, key=lambda x: x[0])]


def attention(nc, name, decayed, keep, dram):
    with ExitStack() as ctx:
        sb = lambda n, s, d: ctx.enter_context(nc.sbuf_tensor(f"{name}_{n}", s, d))
        ps = lambda n, s: ctx.enter_context(nc.psum_tensor(f"{name}_{n}", s, F32))
        sm = phase_semaphores(nc, ctx, name)
        kop = sb("kop", [P, 2, GH, T], F32R)
        qop = sb("qop", [P, 2, GH, T], F32R)
        va = sb("va", [P, 2, BLOCKS, GH, STRIP], F32)
        buffers = 4
        MBANKS, EBANKS = (4, 2) if decayed else (3, 3)
        wt = sb("wt", [P, buffers, GH, CH], F32)
        wd = sb("wd", [P, 2, GH, CH], F32) if decayed else None
        mpart = sb("mpart", [P, NC, NC, UNITS], F32)
        mneg = sb("mneg", [P, NC, UNITS], F32)
        mrow = sb("mrow", [UNITS, NC, P], F32R)
        if decayed:
            fsum, ffactor = (sb(n, [P, NC, NC - 2, UNITS], F32) for n in ("fsum", "ffactor"))
            ftotal, frow = sb("ftotal", [P, NC, UNITS], F32), sb("frow", [UNITS, NC - 2, P], F32)
        y = sb("y", [P, 2, CH], F32)
        pm, pe_, po, px = ps("pm", [P, MBANKS, CH]), ps("ps", [P, EBANKS, CH]), ps("po", [P, CH]), ps("px", [P, CH])

        qk_in = [[sm(f"qk_in{i}{c}") for c in range(NC)] for i in range(2)]
        m_in = [sm(f"m_in{c}") for c in range(NC)]
        v_in = [sm("v_in0"), sm("v_in1")]
        q_padded, k_padded = ([sm(f"{n}{i}") for i in range(2)] for n in ("q_padded", "k_padded"))
        m_scores, m_reduced, m_final = sm("m_scores"), sm("m_reduced"), sm("m_final")
        x_written, x_read, mrow_ready = sm("x_written"), sm("x_read"), sm("mrow_ready")
        e_scores, e_weights, w_decayed = sm("e_scores"), sm("e_weights"), sm("w_decayed")
        f_done, f_diff, f_factor, f_prod, f_total = (sm(n) for n in ("f_done", "f_diff", "f_factor", "f_prod", "f_total"))
        f_out = [sm(f"f_out{c}") for c in range(NC)]
        w_masked, w_turn = sm("w_masked"), sm("w_turn")
        pv_done, o_kept = sm("pv_done"), sm("o_kept")
        y_out = [sm(f"y_out{i}") for i in range(2)]
        block = ctx.enter_context(nc.Block())

        qk_g = dram["qk"].rearrange("b g h q (j d) t -> (b g) h q d j t", d=HD)
        v_g = dram["v"].rearrange("b g c p e -> (b g) p c e")
        far_g = dram["far"].rearrange("b g c u t -> (b g) c u t")
        y_g = dram["y"].rearrange("b g c p t -> (b g) c p t")
        KBS = sum(len(near(c, decayed)) for c in range(NC))
        E_UNITS = GH * KBS
        FARS = [c for c in range(NC) if far(c, decayed)]
        X_USES = NC + len(FARS)
        QK_LOADS = 16 * (2 * PAIRS + 1)
        M_DMAS = 16 * GH
        STEP = attention_plan(True, True, True, decayed)
        FIRST = attention_plan(False, False, True, decayed)
        LAST = attention_plan(True, True, False, decayed)

        def steps(eng, step):
            step(-1, -1, 1, FIRST)
            with eng.Fori(0, GROUPS // 2 - 1) as i:
                for u in range(2):
                    step(2 * i + u, i, u, STEP)
            step(GROUPS - 2, GROUPS // 2 - 1, 0, STEP)
            step(GROUPS - 1, GROUPS // 2 - 1, 1, LAST)

        def x_use(g, c, of_sums):
            return X_USES * g + c + sum(f < c for f in FARS) + of_sums

        def far_left(n):
            def is_far(k):
                per = [UNITS * (c + 1) for c in range(NC)]
                k %= M_UNITS
                for c in range(NC):
                    if k < per[c]:
                        return k % (c + 1) in far(c, decayed)
                    k -= per[c]

            k = n - MBANKS
            return sum(is_far(i) for i in range(k + 1)) if k >= 0 else -sum(is_far(i) for i in range(k + 1, 0))

        def pad(eng, t, par, padded):
            for c in range(NC):
                eng.memset(t[MROW:P, par, :, c * CH:(c + 1) * CH].bitcast(F32), 1.0 if t is kop else 0.0)\
                   .then_inc(padded, 1)

        def maxima(g, i, par, d):
            return (par, i) if d == 0 else (1 - par, i + par)

        @block.sync
        def _(sp):
            for i in range(2):
                sp.sem_inc(y_out[i], 16)
            for c in range(NC):
                sp.sem_inc(m_in[c], M_DMAS)
            for c in FARS:
                sp.sem_inc(f_out[c], 16)

            def load(g, par, first):
                for c in range(NC):
                    cols = slice(c * CH, (c + 1) * CH)
                    for r in range(PAIRS):
                        rows = slice(r * HD, (r + 1) * HD)
                        sp.dma_start(kop[rows, par, :, cols].bitcast(F32), qk_g[g, r % 2, 1, :, :, cols]).then_inc(qk_in[par][c], 16)
                        sp.dma_start(qop[rows, par, :, cols].bitcast(F32), qk_g[g, r // 2, 0, :, :, cols]).then_inc(qk_in[par][c], 16)
                    if first:
                        sp.wait_ge(q_padded[par], c + 1)
                    sp.dma_start(qop[MROW:MROW + 1, par, :, cols].bitcast(F32),
                                 qop[96:97, par, :, cols].bitcast(F32)).then_inc(qk_in[par][c], 16)
                sp.dma_start(va[:, par, :, :, :].rearrange("p (c t) j e -> p c (t j e)", c=NC), v_g[g])\
                  .then_inc(v_in[par], 16)

            def step(g, i, par, plan):
                for item in plan:
                    if item[0] == "MC":
                        _, d, c = item
                        mpar, _ = maxima(g, i, par, d)
                        sp.wait_ge(x_read, x_use(g + d, c, 0) + 2)
                        for j in range(GH):
                            sp.dma_start(qop[MROW:MROW + 1, mpar, j, c * CH:(c + 1) * CH].bitcast(F32),
                                         mrow[TB * j:TB * j + TB, c, :].bitcast(F32)).then_inc(m_in[c], 16)
                    if item[0] == "FC":
                        _, d, c = item
                        sp.wait_ge(x_read, x_use(g + d, c, 1) + 2)
                        sp.dma_start(far_g[g + d, c], frow[:, FARS.index(c), :]).then_inc(f_out[c], 16)
                    if item[0] == "O":
                        c = item[1]
                        sp.wait_ge(o_kept, NC * g + c + 2)
                        sp.dma_start(y_g[g, c], y[:, c % 2, :]).then_inc(y_out[c % 2], 16)
                if plan is STEP and not (isinstance(g, int) and g == GROUPS - 2):
                    sp.wait_ge(e_scores, E_UNITS * (g + 1))
                    sp.wait_ge(pv_done, KBS * (g + 1) + buffers)
                    load(g + 2, par, False)

            load(0, 0, True)
            load(1, 1, True)
            steps(sp, step)
            for i in range(2):
                sp.wait_ge(y_out[i], 16 * (GROUPS * NC // 2 + 1))
            for c in FARS:
                sp.wait_ge(f_out[c], 16 * (GROUPS + 1))

        @block.gpsimd
        def _(pool):
            for t, par, padded in ((kop, 0, k_padded), (qop, 1, q_padded), (kop, 1, k_padded)):
                pad(pool, t, par, padded[par])
            pool.wait_ge(k_padded[1], NC)
            if decayed:
                def step(g, i, par, plan):
                    seen = 0
                    for item in plan:
                        if item[0] != "S":
                            continue
                        _, c, kb, j = item
                        seen += 1
                        kq = (seen - 1) // GH
                        a, z, u = band_columns(c, kb)
                        pool.wait_ge(e_weights, E_UNITS * g + seen + EBANKS)
                        pool.wait_ge(pv_done, KBS * g + kq + 1 + buffers - 2)
                        pool.tensor_tensor(wd[:, kq % 2, j, a:z], wt[:, kq % buffers, j, a:z],
                                           keep["decay"][:, u:u + z - a], ALU.mult).then_inc(w_decayed, 1)

                steps(pool, step)
            else:
                def step(g, i, par, plan):
                    seen = 0
                    for item in plan:
                        if item[0] != "S":
                            continue
                        _, c, kb, j = item
                        seen += 1
                        if kb < TB * c or j < GH - 1:
                            continue
                        pool.wait_ge(e_weights, E_UNITS * g + seen + EBANKS)
                        pool.sem_inc(w_turn, 1)
                        block = wt[:, (seen // GH - 1) % buffers, :, P * (kb - TB * c):P * (kb - TB * c + 1)]
                        pool.affine_select(out=block, in_=block, compare_op=ALU.is_ge, fill=0.0, base=0,
                                           pattern=[[0, GH], [1, P]], channel_multiplier=-1).then_inc(w_masked, 1)

                steps(pool, step)

        @block.scalar
        def _(act):
            act.sem_inc(e_weights, EBANKS)
            act.sem_inc(o_kept, 1)
            act.sem_inc(f_done, MBANKS)

            def step(g, i, par, plan):
                seen = 0
                for item in plan:
                    if item[0] == "S":
                        _, c, kb, j = item
                        a = P * max(0, kb - TB * c)
                        kq = seen // GH
                        act.wait_ge(e_scores, E_UNITS * g + seen + 1)
                        act.wait_ge(pv_done, KBS * g + kq + 1)
                        act.activation(wt[:, kq % buffers, j, a:CH], pe_[:, seen % EBANKS, 0:CH - a], ACT.Exp)\
                           .then_inc(e_weights, 1)
                        seen += 1
                    if item[0] == "FX":
                        _, d, n, c, qb, j, piece = item
                        act.wait_ge(m_reduced, M_UNITS * (g + d) + n + 1 + MBANKS)
                        u = TB * j + qb
                        act.activation(pm[:, n % MBANKS, :], pm[:, n % MBANKS, :], ACT.Exp,
                                       bias=mpart[:, c, piece, u:u + 1],
                                       accum_out=fsum[:, c, piece, u:u + 1]).then_inc(f_done, 1)
                    if item[0] == "FE":
                        _, d, c = item
                        act.wait_ge(f_diff, len(FARS) * (g + d) + FARS.index(c) + 1)
                        n = len(far(c, decayed))
                        act.activation(ffactor[:, c, 0:n, :], ffactor[:, c, 0:n, :], ACT.Exp).then_inc(f_factor, 1)
                    if item[0] == "O":
                        c = item[1]
                        act.wait_ge(pv_done, KBS * g + sum(len(near(a, decayed)) for a in range(c + 1)) + buffers)
                        act.wait_ge(y_out[c % 2], 16 * (2 * g + c // 2 + 1))
                        act.activation(y[:, c % 2, :], po[:, :], ACT.Copy).then_inc(o_kept, 1)

            steps(act, step)

        @block.vector
        def _(dve):
            pad(dve, qop, 0, q_padded[0])
            dve.sem_inc(m_reduced, MBANKS)
            dve.sem_inc(x_read, 1)

            def step(g, i, par, plan):
                for item in plan:
                    if item[0] == "M":
                        _, d, n, c, qb, j, piece = item
                        w = CH if piece < c else P * (qb + 1)
                        dve.wait_ge(m_scores, M_UNITS * (g + d) + n + 1)
                        u = TB * j + qb
                        dve.tensor_reduce(mpart[:, c, piece, u:u + 1], pm[:, n % MBANKS, 0:w],
                                          AX.X, ALU.max, negate=True).then_inc(m_reduced, 1)
                    if item[0] == "MF":
                        _, d, c = item
                        dve.wait_ge(m_reduced, M_UNITS * (g + d) + GH * sum(TB * (a + 1) for a in range(c + 1)) + MBANKS)
                        dve.tensor_reduce(mneg[:, c, :], mpart[:, c, 0:c + 1, :].rearrange("p n u -> p u n"),
                                          AX.X, ALU.min).then_inc(m_final, 1)
                        if c in FARS:
                            dve.wait_ge(m_final, NC * (g + d) + c + 1)
                            for n in far(c, decayed):
                                s = dve.tensor_tensor(ffactor[:, c, n, :], mneg[:, c, :], mpart[:, c, n, :], ALU.subtract)
                            s.then_inc(f_diff, 1)
                    if item[0] == "FM":
                        _, d, c = item
                        n, index = len(far(c, decayed)), len(FARS) * (g + d) + FARS.index(c)
                        dve.wait_ge(f_factor, index + 1)
                        dve.wait_ge(f_done, FAR_UNITS * (g + d) + UNITS * sum(len(far(a, decayed)) for a in range(c + 1)) + MBANKS)
                        dve.tensor_tensor(ffactor[:, c, 0:n, :], ffactor[:, c, 0:n, :], fsum[:, c, 0:n, :], ALU.mult)\
                           .then_inc(f_prod, 1)
                        dve.wait_ge(f_prod, index + 1)
                        dve.tensor_reduce(ftotal[:, c, :], ffactor[:, c, 0:n, :].rearrange("p n u -> p u n"),
                                          AX.X, ALU.add).then_inc(f_total, 1)
                    if item[0] == "FC":
                        _, d, c = item
                        dve.wait_ge(x_written, x_use(g + d, c, 1) + 1)
                        dve.wait_ge(f_out[c], 16 * (g + d + 1))
                        dve.tensor_copy(frow[:, FARS.index(c), :], px[0:UNITS, 0:P]).then_inc(x_read, 1)
                    if item[0] == "MC":
                        _, d, c = item
                        dve.wait_ge(x_written, x_use(g + d, c, 0) + 1)
                        dve.wait_ge(m_in[c], M_DMAS * (g + d + 1))
                        dve.tensor_copy(mrow[:, c, :], px[0:GH * TB, 0:P]).then_inc(x_read, 1)

            steps(dve, step)

        @block.tensor
        def _(pe):
            pe.sem_inc(pv_done, buffers)
            def step(g, i, par, plan):
                e = kq = ones = masked = 0
                for item in plan:
                    if item[0] == "M":
                        _, d, n, c, qb, j, piece = item
                        mpar, before = maxima(g, i, par, d)
                        if (qb, j, piece) == (0, 0, 0):
                            if plan is FIRST:
                                pe.wait_ge(k_padded[0], c + 1)
                                pe.wait_ge(q_padded[0], c + 1)
                            elif plan is STEP and d == 1 and par == 0:
                                pe.wait_ge(k_padded[1], c + 1)
                                pe.wait_ge(q_padded[1], c + 1)
                            pe.wait_ge(qk_in[mpar][c], QK_LOADS * (before + 1))
                        w = CH if piece < c else P * (qb + 1)
                        bank = n % MBANKS
                        pe.wait_ge(m_reduced, M_UNITS * (g + d) + max(n + 1, MBANKS))
                        if FARS:
                            pe.wait_ge(f_done, FAR_UNITS * (g + d) + far_left(n) + MBANKS)
                        q0 = c * CH + qb * P
                        mm = pe.matmul(pm[:, bank, 0:w], qop[:, mpar, j, q0:q0 + P],
                                       kop[:, mpar, j, piece * CH:piece * CH + w], start=True, stop=piece < c)
                        if piece == c:
                            mm = pe.matmul(pm[:, bank, w - P:w], keep["identr"][:, :], keep["mask_q"][:, :],
                                           start=False, stop=True)
                        mm.then_inc(m_scores, 1)
                    if item[0] == "MT":
                        _, d, c = item
                        pe.wait_ge(m_final, NC * (g + d) + c + 1)
                        pe.wait_ge(x_read, x_use(g + d, c, 0) + 1)
                        pe.matmul(px[0:GH * TB, 0:P], mneg[:, c, :], keep["ident"][:, :], start=True, stop=True)\
                          .then_inc(x_written, 1)
                    if item[0] == "FT":
                        _, d, c = item
                        pe.wait_ge(f_total, len(FARS) * (g + d) + FARS.index(c) + 1)
                        pe.wait_ge(x_read, x_use(g + d, c, 1) + 1)
                        pe.matmul(px[0:UNITS, 0:P], ftotal[:, c, :], keep["ident"][:, :], start=True, stop=True)\
                          .then_inc(x_written, 1)
                    if item[0] == "S":
                        _, c, kb, j = item
                        if kb == near(c, decayed)[0] and j == 0:
                            pe.wait_ge(m_in[c], M_DMAS * (g + 2))
                            if c == 0:
                                pe.wait_ge(v_in[par], 16 * (i + 1))
                        a = P * max(0, kb - TB * c)
                        bank = e % EBANKS
                        pe.wait_ge(e_weights, E_UNITS * g + max(e + 1, EBANKS))
                        diagonal = decayed and kb >= TB * c
                        mm = pe.matmul(pe_[:, bank, 0:CH - a], kop[:, par, j, kb * P:(kb + 1) * P],
                                       qop[:, par, j, c * CH + a:(c + 1) * CH], start=True, stop=not diagonal)
                        if diagonal:
                            mm = pe.matmul(pe_[:, bank, 0:P], keep["identr"][:, :], keep["mask_k"][:, :],
                                           start=False, stop=True)
                        mm.then_inc(e_scores, 1)
                        e += 1
                    if item[0] in ("PO", "PV"):
                        _, c, kb = item
                        a = P * max(0, kb - TB * c)
                        last = kb == TB * (c + 1) - 1
                        first = kb == near(c, decayed)[0]
                    if item[0] == "PO":
                        pe.wait_ge(e_weights, E_UNITS * g + GH * (ones + 1) + EBANKS)
                        if first:
                            pe.wait_ge(o_kept, NC * g + c + 1)
                        for j in range(GH):
                            mm = pe.matmul(po[STRIP * j:STRIP * (j + 1), a:CH], keep["ones_strip"][:, :],
                                           wt[:, ones % buffers, j, a:CH], start=first, stop=False)
                        ones += 1
                    if item[0] == "PV" and decayed:
                        pe.wait_ge(w_decayed, E_UNITS * g + GH * (kq + 1))
                        a, z, _ = band_columns(c, kb)
                        for j in range(GH):
                            mm = pe.matmul(po[STRIP * j:STRIP * (j + 1), a:z], va[:, par, kb, j, :],
                                           wd[:, kq % 2, j, a:z], start=False, stop=last)
                    if item[0] == "PV" and not decayed:
                        pe.wait_ge(e_weights, E_UNITS * g + GH * (kq + 1) + EBANKS)
                        if first:
                            pe.wait_ge(o_kept, NC * g + c + 1)
                        if kb >= TB * c:
                            masked += 1
                            pe.wait_ge(w_masked, NC * TB * g + masked)
                        for j in range(GH):
                            mm = pe.matmul(po[STRIP * j:STRIP * (j + 1), a:CH], va[:, par, kb, j, :],
                                           wt[:, kq % buffers, j, a:CH], start=first, stop=last)
                    if item[0] == "PV":
                        mm.then_inc(pv_done, 1)
                        kq += 1

            steps(pe, step)


def band_columns(c, kb):
    a = P * max(0, kb - TB * c)
    z = min(CH, P * (kb - TB * c + BAND + 1))
    return a, z, P * (TB * c - kb) + a


def output_projection(nc, name, x_src, x_dst, xn_dst, w, norm, decayed, keep, dram):
    with ExitStack() as ctx:
        sb = lambda n, s, d: ctx.enter_context(nc.sbuf_tensor(f"{name}_{n}", s, d))
        sm = phase_semaphores(nc, ctx, name)
        wp = sb("wp", [P, NG, D], F32)
        gamma, beta = sb("gamma", [P, D], F32), sb("beta", [P, D], F32)
        y = sb("y", [P, 2, NG, CH], F32)
        yn = sb("yn", [P, 2, NG, CH], F32)
        sums = sb("sums", [P, 2, SUMS], F32)
        far_sums = sb("far_sums", [P, 2, SUMS], F32)
        part = sb("part", [P, 2, SUMS], F32)
        spread = sb("spread", [P, 2, NG, CH], F32)
        x = sb("x", [P, 2, TB, D], F32)
        xb = sb("xb", [P, 2, TB, D], F32)
        zg = sb("zg", [P, 2, TB, D], F32)
        xo = sb("xo", [P, 2, TB, D], F32)
        xn = sb("xn", [P, 2, TB, D], F32)
        stats = sb("stats", [P, TB, 6], F32)
        mean, half = sb("mean", [P, 2, TB], F32), sb("half", [P, 2, TB], F32)
        var, sd, rs, shift = (sb(n, [P, 2, TB], F32) for n in ("var", "sd", "rs", "shift"))
        pp = ctx.enter_context(nc.psum_tensor(f"{name}_pp", [P, 2, TB, D], F32))
        zeroed, ones_in, w_in = sm("zeroed"), sm("ones_in"), sm("w_in")
        y_in, x_in = ([sm(f"{n}{i}") for i in range(2)] for n in ("y_in", "x_in"))
        s_in, r_out, r_in = ([sm(f"{n}{i}") for i in range(2)] for n in ("s_in", "r_out", "r_in"))
        f_in, summed = [sm(f"f_in{c}") for c in range(NC)], sm("summed")
        part_ready, yn_ready = sm("part_ready"), sm("yn_ready")
        projected, p_read, chain = sm("projected"), sm("p_read"), sm("chain")
        var_ready, sd_ready, xb_ready = sm("var_ready"), sm("sd_ready"), sm("xb_ready")
        xo_ready, xn_ready, shift_ready = sm("xo_ready"), sm("xn_ready"), sm("shift_ready")
        stored = [sm(f"stored{i}") for i in range(2)]
        block = ctx.enter_context(nc.Block())
        NW = 16 * (GH + 3 * bool(norm))
        NORMS = 2 if norm else 1

        @block.sync
        def _(sp):
            for par in range(2):
                sp.sem_inc(r_out[par], 16)

            def load_weights():
                sp.wait_ge(zeroed, 1)
                for j in range(GH):
                    sp.dma_start(wp[STRIP * j:STRIP * j + HD, :, :],
                                 w.rearrange("(g j d) n -> j d g n", j=GH, d=HD)[j]).then_inc(w_in, 16)
                if norm:
                    sp.dma_start(wp[HD:HD + 1, 0, :], row_of(norm[0])).then_inc(w_in, 16)
                    for t, src in zip((gamma, beta), norm[1:]):
                        sp.dma_start(t[:, :], row_of(src).to_broadcast([P, D])).then_inc(w_in, 16)

            def load_sums(b, c):
                G, par = NC * b + c, c % 2
                sp.wait_ge(part_ready, G + 1)
                for g in range(NG):
                    src = dram["y"][b + c // NC, g, c % NC].rearrange("(j r) (s t) -> r j s t", j=GH, t=SUMS)[HD]
                    sp.dma_start(sums[g * STRIP:(g + 1) * STRIP, par, :], src).then_inc(s_in[par], 16)
                if far(c % NC, decayed):
                    src = dram["far"][b + c // NC, :, c % NC].rearrange("g u (h t) -> g (u h) t", t=SUMS)
                    sp.dma_start(far_sums[:, par, :], src).then_inc(f_in[c % NC], 16)

            def load_y(b, c):
                G, par = NC * b + c, c % 2
                sp.wait_ge(yn_ready, G + 1)
                src = dram["y"][b + c // NC, :, c % NC].rearrange("g (j r) t -> j r g t", j=GH)
                for j in range(GH):
                    sp.dma_start(y[STRIP * j:STRIP * j + HD, par, :, :], src[j, 0:HD]).then_inc(y_in[par], 16)

            def store_part(b, c):
                sp.wait_ge(part_ready, NC * b + c + 3)
                sp.dma_start(at(dram["part"], b, c), part[:, c % 2, :]).then_inc(r_out[c % 2], 16)

            def load_spread(b, c):
                G, par = NC * b + c, c % 2
                part_d = at(dram["part"], b, c)
                sp.wait_ge(yn_ready, G + 1)
                sp.wait_ge(r_out[par], 16 * (2 * b + c // 2 + 2))
                for j in range(GH):
                    src = part_d.rearrange("(g j s) t -> j g (s t)", j=GH, g=NG)[j]
                    src = src.rearrange("(o g) q -> o g q", o=1).to_broadcast([HD, NG, CH])
                    sp.dma_start(spread[STRIP * j:STRIP * j + HD, par, :, :], src).then_inc(r_in[par], 16)

            def load_x(b, c):
                G, par = NC * b + c, c % 2
                sp.wait_ge(xo_ready, G + 1)
                sp.dma_start(x[:, par, :, :], at(x_src, b, c)).then_inc(x_in[par], 16)

            def body(b, last):
                for c in range(NC):
                    if not last or c + 2 < NC:
                        load_y(b, c + 2)
                    if not last or c + 3 < NC:
                        load_sums(b, c + 3)
                    if not last or c + 2 < NC:
                        store_part(b, c + 2)
                        load_spread(b, c + 2)
                        load_x(b, c + 2)

            load_sums(0, 0)
            store_part(0, 0)
            load_sums(0, 1)
            sp.wait_ge(ones_in, 2)
            load_y(0, 0)
            load_spread(0, 0)
            load_weights()
            store_part(0, 1)
            load_sums(0, 2)
            sp.wait_ge(ones_in, 4)
            load_y(0, 1)
            load_spread(0, 1)
            load_x(0, 0)
            load_x(0, 1)
            sequences(sp, body)
        @block.gpsimd
        def _(pool):
            pool.memset(y[:, 0, :, :], 1.0).then_inc(ones_in, 1)
            pool.memset(spread[:, 0, :, :], 1.0).then_inc(ones_in, 1)
            pool.memset(wp[:, :, :], 0.0).then_inc(zeroed, 1)
            pool.memset(y[:, 1, :, :], 1.0).then_inc(ones_in, 1)
            pool.memset(spread[:, 1, :, :], 1.0).then_inc(ones_in, 1)
            if norm:
                pool.wait_ge(w_in, NW)
                with pool.Fori(0, B) as b:
                    for c in range(NC):
                        G, par = NC * b + c, c % 2
                        pool.wait_ge(x_in[par], 16 * (2 * b + c // 2 + 1))
                        pool.wait_ge(xo_ready, G + 1)
                        for t in range(TB):
                            s = pool.tensor_tensor(xb[:, par, t, :], x[:, par, t, :], beta[:, :], ALU.add)
                        s.then_inc(xb_ready, 1)

        @block.tensor
        def _(pe):
            pe.sem_inc(projected, 2)
            pe.wait_ge(w_in, NW)
            with pe.Fori(0, B) as b:
                for c in range(NC):
                    G, par = NC * b + c, c % 2
                    pe.wait_ge(yn_ready, G + 3)
                    pe.wait_ge(p_read if norm else xo_ready, G + 1)
                    for t in range(TB):
                        for g in range(NG):
                            mm = pe.matmul(pp[:, par, t, :], yn[:, par, g, t * P:(t + 1) * P], wp[:, g, :],
                                           start=(g == 0), stop=(g == NG - 1))
                    mm.then_inc(projected, 1)

        @block.scalar
        def _(act):
            for par in range(2):
                act.sem_inc(stored[par], 32)
            with act.Fori(0, B) as b:
                for c in range(NC):
                    G, par = NC * b + c, c % 2

                    def root(n):
                        act.wait_ge(var_ready, NORMS * G + n + 1)
                        act.activation(sd[:, par, :], var[:, par, :], ACT.Sqrt).then_inc(sd_ready, 1)

                    if norm:
                        root(0)
                    act.wait_ge(xo_ready, G + 3)
                    act.dma_start(x_dst[b, c], xo[:, par, :, :]).then_inc(stored[par], 16)
                    root(NORMS - 1)
                    act.wait_ge(shift_ready, G + 1)
                    for t in range(TB):
                        s = act.activation(xn[:, par, t, :], xo[:, par, t, :], ACT.Identity,
                                           bias=shift[:, par, t:t + 1], scale=rs[:, par, t:t + 1])
                    s.then_inc(xn_ready, 1)
                    act.wait_ge(xn_ready, G + 1)
                    act.dma_start(xn_dst[b, c], xn[:, par, :, :]).then_inc(stored[par], 16)
            for par in range(2):
                act.wait_ge(stored[par], 32 * (B * NC // 2 + 1))

        @block.vector
        def _(dve):
            dve.sem_inc(p_read, 2)
            dve.sem_inc(xo_ready, 2)

            def moments(G, par, src, n):
                first = 4 * (NORMS * G + n) + 1
                for t in range(TB):
                    s = dve.bn_stats(stats[:, t, :], src[:, par, t, :])
                s.then_inc(chain, 1)
                dve.wait_ge(chain, first)
                halves_sums(dve, stats, mean[:, par, :], half).then_inc(chain, 1)
                dve.wait_ge(chain, first + 1)
                halves_terms(dve, mean[:, par, :], half).then_inc(chain, 1)
                dve.wait_ge(chain, first + 2)
                halves_variance(dve, var[:, par, :], half).then_inc(var_ready, 1)
                dve.wait_ge(sd_ready, NORMS * G + n + 1)
                dve.reciprocal(rs[:, par, :], sd[:, par, :]).then_inc(chain, 1)
                dve.wait_ge(chain, first + 3)

            def invert(b, c):
                G, par = NC * b + c, c % 2
                dve.wait_ge(s_in[par], 16 * NG * (2 * b + c // 2 + 1))
                dve.wait_ge(r_out[par], 16 * (2 * b + c // 2 + 1))
                if far(c % NC, decayed):
                    dve.wait_ge(f_in[c % NC], 16 * (b + c // NC + 1))
                    dve.tensor_tensor(sums[:, par, :], sums[:, par, :], far_sums[:, par, :], ALU.add).then_inc(summed, 1)
                    far_chunks = [a for a in range(NC) if far(a, decayed)]
                    dve.wait_ge(summed, len(far_chunks) * (b + c // NC) + far_chunks.index(c % NC) + 1)
                dve.reciprocal(part[:, par, :], sums[:, par, :]).then_inc(part_ready, 1)

            def divide(b, c):
                G, par = NC * b + c, c % 2
                dve.wait_ge(y_in[par], 16 * GH * (2 * b + c // 2 + 1))
                dve.wait_ge(r_in[par], 16 * GH * (2 * b + c // 2 + 1))
                dve.wait_ge(projected, G + 1)
                dve.tensor_tensor(yn[:, par, :, :], y[:, par, :, :], spread[:, par, :, :], ALU.mult)\
                   .then_inc(yn_ready, 1)

            dve.sem_inc(part_ready, 2)
            dve.sem_inc(yn_ready, 2)

            def body(b, last):
                for c in range(NC):
                    G, par = NC * b + c, c % 2
                    if not last or c + 1 < NC:
                        divide(b, c + 1)
                    if not last or c + 2 < NC:
                        invert(b, c + 2)
                    dve.wait_ge(projected, G + 3)
                    if norm:
                        moments(G, par, pp, 0)
                        for t in range(TB):
                            s = dve.scalar_tensor_tensor(out=zg[:, par, t, :], in0=pp[:, par, t, :],
                                                         scalar=mean[:, par, t:t + 1], in1=gamma[:, :],
                                                         op0=ALU.subtract, op1=ALU.mult)
                        s.then_inc(p_read, 1)
                        dve.wait_ge(p_read, G + 3)
                        dve.wait_ge(xb_ready, G + 1)
                        dve.wait_ge(stored[par], 32 * (2 * b + c // 2 + 1))
                        for t in range(TB):
                            s = dve.scalar_tensor_tensor(out=xo[:, par, t, :], in0=zg[:, par, t, :],
                                                         scalar=rs[:, par, t:t + 1], in1=xb[:, par, t, :],
                                                         op0=ALU.mult, op1=ALU.add)
                        s.then_inc(xo_ready, 1)
                    else:
                        dve.wait_ge(x_in[par], 16 * (2 * b + c // 2 + 1))
                        dve.wait_ge(stored[par], 32 * (2 * b + c // 2 + 1))
                        for t in range(TB):
                            s = dve.tensor_tensor(xo[:, par, t, :], pp[:, par, t, :], x[:, par, t, :], ALU.add)
                        s.then_inc(xo_ready, 1)
                    dve.wait_ge(xo_ready, G + 3)
                    moments(G, par, xo, NORMS - 1)
                    dve.scalar_tensor_tensor(out=shift[:, par, :], in0=mean[:, par, :], scalar=-1.0,
                                             in1=rs[:, par, :], op0=ALU.mult, op1=ALU.mult).then_inc(shift_ready, 1)

            invert(0, 0)
            invert(0, 1)
            divide(0, 0)
            dve.wait_ge(w_in, NW)
            sequences(dve, body)


def feed_forward(nc, name, x_src, xn_src, dst, keep, dram):
    with ExitStack() as ctx:
        sb = lambda n, s, d: ctx.enter_context(nc.sbuf_tensor(f"{name}_{n}", s, d))
        ps = lambda n, s: ctx.enter_context(nc.psum_tensor(f"{name}_{n}", s, F32))
        sm = phase_semaphores(nc, ctx, name)
        w1s, w2s = sb("w1_signs", [P, KT, FF], F32R), sb("w2_signs", [P, HT, D], F32R)
        w_in = sm("w_in")
        GB = 4
        x = sb("x", [P, 2, TB, D], F32)
        xn = sb("xn", [P, 2, TB, D], F32)
        xt_hi, xt_lo = sb("xt_hi", [P, 2, KT, CH], F32R), sb("xt_lo", [P, 2, KT, CH], F32R)
        g = sb("g", [P, GB, CH], F32)
        g_hi, g_lo = sb("g_hi", [P, GB, CH], F32R), sb("g_lo", [P, GB, CH], F32R)
        o = sb("o", [P, KT, CH], F32)
        xo = sb("xo", [P, 2, TB, D], F32)
        pt, ph, po, pb = ps("pt", [P, KT, CH]), ps("ph", [P, 2, CH]), ps("po", [P, KT, CH]), ps("pb", [P, TB, D])
        xn_in, x_in = ([sm(f"{n}{i}") for i in range(2)] for n in ("xn_in", "x_in"))
        turned, hi_ready, lo_ready = sm("turned"), sm("hi_ready"), sm("lo_ready")
        h_done, g_ready, g_hi_ready, g_lo_ready = sm("h_done"), sm("g_ready"), sm("g_hi_ready"), sm("g_lo_ready")
        g_used, o_kept, back, xo_ready = sm("g_used"), sm("o_kept"), sm("back"), sm("xo_ready")
        stored = [sm(f"stored{i}") for i in range(2)]
        block = ctx.enter_context(nc.Block())

        @block.sync
        def _(sp):
            for par in range(2):
                sp.sem_inc(stored[par], 16)

            def store(b, c):
                sp.wait_ge(xo_ready, NC * b + c + 3)
                sp.dma_start(dst[b, c], xo[:, c % 2, :, :]).then_inc(stored[c % 2], 16)

            def load_xn(b, c):
                G, par = NC * b + c, c % 2
                sp.wait_ge(turned, G + 1)
                sp.dma_start(xn[:, par, :, :], at(xn_src, b, c)).then_inc(xn_in[par], 16)

            def load_x(b, c):
                G, par = NC * b + c, c % 2
                sp.wait_ge(xo_ready, G + 1)
                sp.dma_start(x[:, par, :, :], at(x_src, b, c)).then_inc(x_in[par], 16)

            def body(b, last):
                for c in range(NC):
                    follows = not last or c + 2 < NC
                    if follows:
                        load_xn(b, c + 2)
                    store(b, c)
                    if follows:
                        load_x(b, c + 2)

            load_xn(0, 0)
            sp.dma_start(w1s[:, :, :].bitcast(F32), dram["w1s"]).then_inc(w_in, 16)
            sp.dma_start(w2s[:, :, :].bitcast(F32), dram["w2s"]).then_inc(w_in, 16)
            load_xn(0, 1)
            load_x(0, 0)
            load_x(0, 1)
            sequences(sp, body)
            for par in range(2):
                sp.wait_ge(stored[par], 16 * (B * NC // 2 + 1))

        @block.tensor
        def _(pe):
            pe.sem_inc(turned, 2)
            pe.sem_inc(g_used, GB)
            pe.sem_inc(back, 1)

            def turn(b, c):
                G, par = NC * b + c, c % 2
                pe.wait_ge(xn_in[par], 16 * (2 * b + c // 2 + 1))
                pe.wait_ge(lo_ready, G + 1)
                for t in range(TB):
                    for kt in range(KT):
                        mm = pe.transpose(pt[:, kt, t * P:(t + 1) * P], xn[:, par, t, kt * P:(kt + 1) * P],
                                          keep["ident"][:, :])
                mm.then_inc(turned, 1)

            def hidden(b, c, h):
                G, par = NC * b + c, c % 2
                pe.wait_ge(g_ready, HT * G + h + 1)
                n = 0
                for kt in range(KT):
                    for part in (xt_hi, xt_lo):
                        mm = pe.matmul(ph[:, h % 2, :], w1s[:, kt, h * P:(h + 1) * P], part[:, par, kt, :],
                                       start=(n == 0), stop=(n == 2 * KT - 1))
                        n += 1
                mm.then_inc(h_done, 1)

            def output(b, c, h):
                G = NC * b + c
                pe.wait_ge(g_lo_ready, HT * G + h + GB + 1)
                if h == 0:
                    pe.wait_ge(o_kept, G + 1)
                for part, ready in ((g_hi, g_hi_ready), (g_lo, g_lo_ready)):
                    for kt in range(KT):
                        mm = pe.matmul(po[:, kt, :], w2s[:, h, kt * P:(kt + 1) * P],
                                       part[:, h % GB, :],
                                       start=(h == 0 and part is g_hi), stop=(h == HT - 1 and part is g_lo))
                mm.then_inc(g_used, 1)

            def turn_back(b, c):
                G = NC * b + c
                pe.wait_ge(o_kept, G + 2)
                pe.wait_ge(xo_ready, G + 2)
                for t in range(TB):
                    for kt in range(KT):
                        mm = pe.transpose(pb[:, t, kt * P:(kt + 1) * P], o[:, kt, t * P:(t + 1) * P],
                                          keep["ident"][:, :])
                mm.then_inc(back, 1)

            def begin(b, c):
                G = NC * b + c
                pe.wait_ge(hi_ready, G + 1)
                pe.wait_ge(lo_ready, G + 2)

            def body(b, last):
                for c in range(NC):
                    follows = not last or c + 1 < NC
                    for h in range(HT):
                        if 1 <= h < HT - 2:
                            hidden(b, c, h + 2)
                        elif h >= HT - 2 and follows:
                            if h == HT - 2:
                                begin(b, c + 1)
                            hidden(b, c + 1, h + 2 - HT)
                        output(b, c, h)
                        if h == 2 and follows:
                            turn(b, c + 1)
                    if follows:
                        hidden(b, c + 1, 2)
                    turn_back(b, c)

            turn(0, 0)
            begin(0, 0)
            pe.wait_ge(w_in, 32)
            for h in range(EARLY):
                hidden(0, 0, h)
            sequences(pe, body)

        @block.scalar
        def _(act):
            act.sem_inc(g_ready, 2)
            act.sem_inc(o_kept, 1)

            def parts(b, c):
                G, par = NC * b + c, c % 2
                act.wait_ge(turned, G + 3)
                act.activation(xt_hi[:, par, :, :], pt[:, :, :], ACT.Copy).then_inc(hi_ready, 1)

            def leave(b, c):
                G = NC * b + c
                act.wait_ge(g_used, HT * G + HT + GB)
                act.wait_ge(back, G + 1)
                for kt in range(KT):
                    s = act.activation(o[:, kt, :], po[:, kt, :], ACT.Identity, bias=keep["b2"][:, kt:kt + 1],
                                       scale=keep["alpha2"][:, kt:kt + 1])
                s.then_inc(o_kept, 1)

            def hidden(b, c, h):
                G = NC * b + c
                act.wait_ge(h_done, HT * G + h + 1)
                act.wait_ge(g_lo_ready, HT * G + h + 1)
                act.activation(g[:, h % GB, :], ph[:, h % 2, :], ACT.Gelu, bias=keep["b1"][:, h:h + 1],
                               scale=keep["alpha1"][:, h:h + 1]).then_inc(g_ready, 1)

            def body(b, last):
                for c in range(NC):
                    follows = not last or c + 1 < NC
                    for h in range(EARLY, HT):
                        hidden(b, c, h)
                        if h == 5 and follows:
                            parts(b, c + 1)
                    for h in range(EARLY):
                        if h == EARLY - 1:
                            leave(b, c)
                        if follows:
                            hidden(b, c + 1, h)

            parts(0, 0)
            for h in range(EARLY):
                hidden(0, 0, h)
            sequences(act, body)

        @block.vector
        def _(dve):
            dve.sem_inc(lo_ready, 1)
            dve.sem_inc(g_lo_ready, GB)
            dve.sem_inc(xo_ready, 2)

            def add(b, c):
                G, par = NC * b + c, c % 2
                dve.wait_ge(back, G + 2)
                dve.wait_ge(x_in[par], 16 * (2 * b + c // 2 + 1))
                dve.wait_ge(stored[par], 16 * (2 * b + c // 2 + 1))
                dve.tensor_tensor(xo[:, par, :, :], pb[:, :, :], x[:, par, :, :], ALU.add).then_inc(xo_ready, 1)

            def parts(b, c):
                G, par = NC * b + c, c % 2
                dve.wait_ge(hi_ready, G + 1)
                dve.tensor_tensor(xt_lo[:, par, :, :], pt[:, :, :], xt_hi[:, par, :, :].bitcast(F32),
                                  ALU.subtract).then_inc(lo_ready, 1)

            def split(b, c, h):
                G = NC * b + c
                dve.wait_ge(g_ready, HT * G + h + 3)
                dve.wait_ge(g_used, HT * G + h + 1)
                dve.tensor_copy(g_hi[:, h % GB, :], g[:, h % GB, :]).then_inc(g_hi_ready, 1)
                dve.wait_ge(g_hi_ready, HT * G + h + 1)
                dve.tensor_tensor(g_lo[:, h % GB, :], g[:, h % GB, :], g_hi[:, h % GB, :].bitcast(F32),
                                  ALU.subtract).then_inc(g_lo_ready, 1)

            def body(b, last):
                for c in range(NC):
                    follows = not last or c + 1 < NC
                    for h in range(EARLY, HT):
                        split(b, c, h)
                        if h == 5 and follows:
                            parts(b, c + 1)
                    if follows:
                        for h in range(EARLY):
                            split(b, c + 1, h)
                    add(b, c)

            parts(0, 0)
            for h in range(EARLY):
                split(0, 0, h)
            sequences(dve, body)


INPUTS = ["L0_attn_a_x", "L0_attn_a_W_attn", "L0_attn_a_W_proj", "L0_attn_b_Wq", "L0_attn_b_bq", "L0_attn_b_Wk",
          "L0_attn_b_bk", "L0_attn_b_Wv", "L0_attn_b_bv", "L0_attn_b_Wo", "L0_attn_b_bo", "L0_attn_b_gamma",
          "L0_attn_b_beta", "L0_ffn_w1", "L0_ffn_b1", "L0_ffn_w2", "L0_ffn_b2"]


def build(nc, t, decay, out):
    def chunks(a):
        return a.rearrange("b (c t p) d -> b c p t d", t=TB, p=P)

    with ExitStack() as ctx:
        def dram(n, shape, dt):
            return nc.dram_tensor(n, shape, dt, kind="Internal").ap()

        def sb(n, shape, dt):
            return ctx.enter_context(nc.sbuf_tensor(n, shape, dt))

        x = [chunks(t["L0_attn_a_x"])] + [chunks(dram(f"x{i}", (B, T, D), F32)) for i in range(1, 4)] + [chunks(out)]
        xn = chunks(dram("xn", (B, T, D), F32))
        scratch = {
            "qk": dram("qk", (B, NG, 2, 2, GH * HD, T), F32),
            "v": dram("v", (B, NG, NC, P, TB * GH * STRIP), F32),
            "y": dram("y", (B, NG, NC, P, CH), F32),
            "far": dram("far", (B, NG, NC, UNITS, P), F32),
            "w1s": dram("w1s", (P, KT, FF), F32), "w2s": dram("w2s", (P, HT, D), F32),
            "part": dram("part", (B, NC, P, SUMS), F32),
        }
        keep = {
            "ident": sb("ident", [P, P], F32), "identr": sb("identr", [P, P], F32R),
            "mask_q": sb("mask_q", [P, P], F32R), "mask_k": sb("mask_k", [P, P], F32R),
            "ones_strip": sb("ones_strip", [P, STRIP], F32),
            "decay": sb("decay", [P, DECAY_COLS], F32),
            "alpha1": sb("alpha1", [P, HT], F32), "alpha2": sb("alpha2", [P, KT], F32),
            "b1": sb("b1", [P, HT], F32), "b2": sb("b2", [P, KT], F32),
        }
        ffn = {"w1": t["L0_ffn_w1"], "b1": t["L0_ffn_b1"], "w2": t["L0_ffn_w2"], "b2": t["L0_ffn_b2"], "decay": decay}
        setup(nc, ffn, keep, scratch)
        projections(nc, "qkv_a", x[0], [(t["L0_attn_a_W_attn"], (0, 3 * D))], None, False, keep, scratch)
        attention(nc, "att_a", True, keep, scratch)
        output_projection(nc, "out_a", x[0], x[1], xn, t["L0_attn_a_W_proj"], None, True, keep, scratch)
        feed_forward(nc, "ffn_a", x[1], xn, x[2], keep, scratch)
        projections(nc, "qkv_b", x[2], [(t[f"L0_attn_b_W{n}"], (i * D, (i + 1) * D)) for i, n in enumerate("qkv")],
                    [t[f"L0_attn_b_b{n}"] for n in "qkv"], True, keep, scratch)
        attention(nc, "att_b", False, keep, scratch)
        output_projection(nc, "out_b", x[2], x[3], xn, t["L0_attn_b_Wo"],
                          [t[f"L0_attn_b_{n}"] for n in ("bo", "gamma", "beta")], False, keep, scratch)
        feed_forward(nc, "ffn_b", x[3], xn, x[4], keep, scratch)


def kernel(**inputs):
    import concourse.bacc as bacc
    from concourse.bass_utils import run_bass_kernel_spmd

    nc = bacc.Bacc("TRN2", target_bir_lowering=False, num_devices=1)
    arrays = {f"in_{n}": np.ascontiguousarray(inputs[n]) for n in INPUTS}
    t = {n: nc.dram_tensor(f"in_{n}", arrays[f"in_{n}"].shape, F32, kind="ExternalInput").ap() for n in INPUTS}
    arrays["decay_table"] = decay_table()
    decay = nc.dram_tensor("decay_table", arrays["decay_table"].shape, F32, kind="ExternalInput").ap()
    out = nc.dram_tensor("out", (B, T, D), F32, kind="ExternalOutput").ap()
    nc.disable_value_cache = True
    build(nc, t, decay, out)
    return run_bass_kernel_spmd(nc, [arrays], core_ids=[0]).results[0]["out"]
```
